# Optimizing a Trainium2 kernel written in Bass

```python
import numpy as np
import jax
import jax.numpy as jnp

def _softmax(x, axis=-1):
    return jax.nn.softmax(x, axis=axis)

def _gelu(x):
    return jax.nn.gelu(x, approximate=True)

def _silu(x):
    return jax.nn.silu(x)

def _sigmoid(x):
    return jax.nn.sigmoid(x)

def _layernorm(x, axis=-1, eps=1e-05):
    m = jnp.mean(x, axis=axis, keepdims=True)
    v = jnp.var(x, axis=axis, keepdims=True)
    return (x - m) / jnp.sqrt(v + eps)

def _scatter_add(tgt, idx, src, axis=0):
    return tgt.at[idx].add(src)

def _segment_sum(src, seg, n):
    return jax.ops.segment_sum(src, seg, n)
kernel_name = 'mk_seq_postln_d1_jaxref_r8_f10af3'

def setup_inputs(seed: int=0):
    np.random.seed(seed)
    _w = jnp.asarray

    def _L0_attn_setup():
        import jax, jax.numpy as jnp
        import numpy as np
        B, L, E, H = (2, 512, 128, 16)
        D = E // H
        CHUNK = 32

        def _linear_attention(x, W_qkv, W_out):
            Bz, Lz, Ez = x.shape
            scale = D ** (-0.5)
            qkv = x @ W_qkv.T
            qkv = qkv.reshape(Bz, Lz, 3, H, D).transpose(2, 0, 3, 1, 4)
            q, k, v = (qkv[0], qkv[1], qkv[2])
            q = (jax.nn.elu(q) + 1.0) * scale
            k = jax.nn.elu(k) + 1.0
            nc = Lz // CHUNK

            def to_chunks(t):
                return t.reshape(Bz, H, nc, CHUNK, D).transpose(2, 0, 1, 3, 4)
            qc, kc, vc = (to_chunks(q), to_chunks(k), to_chunks(v))
            causal = jnp.tril(jnp.ones((CHUNK, CHUNK), dtype=x.dtype))

            def step(carry, inp):
                S, Z = carry
                qi, ki, vi = inp
                attn = jnp.einsum('bhld,bhmd->bhlm', qi, ki) * causal
                num = jnp.einsum('bhlm,bhme->bhle', attn, vi) + jnp.einsum('bhld,bhde->bhle', qi, S)
                den = attn.sum(-1) + jnp.einsum('bhld,bhd->bhl', qi, Z)
                S = S + jnp.einsum('bhmd,bhme->bhde', ki, vi)
                Z = Z + ki.sum(axis=2)
                return ((S, Z), (num, den))
            S0 = jnp.zeros((Bz, H, D, D), dtype=x.dtype)
            Z0 = jnp.zeros((Bz, H, D), dtype=x.dtype)
            _, (num, den) = jax.lax.scan(step, (S0, Z0), (qc, kc, vc))
            num = num.transpose(1, 2, 0, 3, 4).reshape(Bz, H, Lz, D)
            den = den.transpose(1, 2, 0, 3).reshape(Bz, H, Lz)
            den = jnp.maximum(den, 1e-06)
            out = num / den[..., None]
            out = out.transpose(0, 2, 1, 3).reshape(Bz, Lz, Ez)
            return out @ W_out.T
        key = jax.random.key(seed)
        k1, k2, k3 = jax.random.split(key, 3)
        x = jax.random.normal(k1, (B, L, E), dtype=jnp.float32)
        W_qkv = jax.random.normal(k2, (3 * E, E), dtype=jnp.float32) * 0.02
        W_out = jax.random.normal(k3, (E, E), dtype=jnp.float32) * 0.02
        return {'x': x, 'W_qkv': W_qkv, 'W_out': W_out}
    _L0_attn_in = _L0_attn_setup()

    def _L0_ffn_setup():
        import jax, jax.numpy as jnp
        import numpy as np
        H = 128
        I = 88
        E = 64
        TOP_K = 8
        NG = 8
        TOPK_GROUP = 4
        N_SHARED = 2
        ROUTED_SCALE = 2.5
        S_I = I * N_SHARED

        def _route(x, gate_w, gate_bias):
            T = x.shape[0]
            logits = x @ gate_w.T
            scores = jax.nn.sigmoid(logits)
            scores_for_choice = scores + gate_bias[None, :]
            grp = scores_for_choice.reshape(T, NG, E // NG)
            group_scores = jnp.sum(jax.lax.top_k(grp, 2)[0], axis=-1)
            _, gidx = jax.lax.top_k(group_scores, TOPK_GROUP)
            gmask = jnp.zeros((T, NG), dtype=scores.dtype).at[jnp.arange(T)[:, None], gidx].set(1.0)
            emask = jnp.repeat(gmask, E // NG, axis=1)
            masked = jnp.where(emask > 0, scores_for_choice, 0.0)
            _, topk_idx = jax.lax.top_k(masked, TOP_K)
            topk_w = jnp.take_along_axis(scores, topk_idx, axis=1)
            topk_w = topk_w / (jnp.sum(topk_w, axis=-1, keepdims=True) + 1e-20)
            topk_w = topk_w * ROUTED_SCALE
            rw = jnp.zeros((T, E), dtype=scores.dtype).at[jnp.arange(T)[:, None], topk_idx].add(topk_w)
            return rw

        def _mlp(x, gw, uw, dw):
            return jax.nn.silu(x @ gw.T) * (x @ uw.T) @ dw.T
        key = jax.random.key(seed)
        ks = jax.random.split(key, 10)
        sc = 0.02
        return {'hidden_states': jax.random.normal(ks[0], (1, 128, H), dtype=jnp.float32), 'gate_w': sc * jax.random.normal(ks[1], (E, H), dtype=jnp.float32), 'gate_bias': sc * jax.random.normal(ks[2], (E,), dtype=jnp.float32), 'Wg': sc * jax.random.normal(ks[3], (E, I, H), dtype=jnp.float32), 'Wu': sc * jax.random.normal(ks[4], (E, I, H), dtype=jnp.float32), 'Wd': sc * jax.random.normal(ks[5], (E, H, I), dtype=jnp.float32), 'Sg': sc * jax.random.normal(ks[6], (S_I, H), dtype=jnp.float32), 'Su': sc * jax.random.normal(ks[7], (S_I, H), dtype=jnp.float32), 'Sd': sc * jax.random.normal(ks[8], (H, S_I), dtype=jnp.float32)}
    _L0_ffn_in = _L0_ffn_setup()
    _d = {'L0_attn_x': _L0_attn_in['x'], 'L0_attn_W_qkv': _L0_attn_in['W_qkv'], 'L0_attn_W_out': _L0_attn_in['W_out'], 'L0_ffn_gate_w': _L0_ffn_in['gate_w'], 'L0_ffn_gate_bias': _L0_ffn_in['gate_bias'], 'L0_ffn_Wg': _L0_ffn_in['Wg'], 'L0_ffn_Wu': _L0_ffn_in['Wu'], 'L0_ffn_Wd': _L0_ffn_in['Wd'], 'L0_ffn_Sg': _L0_ffn_in['Sg'], 'L0_ffn_Su': _L0_ffn_in['Su'], 'L0_ffn_Sd': _L0_ffn_in['Sd']}
    _x0 = _d['L0_attn_x']
    _d['L0_attn_x'] = jax.random.normal(jax.random.fold_in(jax.random.key(seed), 1), (4, 512, 128), dtype=_x0.dtype)
    del _x0
    return _d

def reference(L0_attn_x, L0_attn_W_qkv, L0_attn_W_out, L0_ffn_gate_w, L0_ffn_gate_bias, L0_ffn_Wg, L0_ffn_Wu, L0_ffn_Wd, L0_ffn_Sg, L0_ffn_Su, L0_ffn_Sd):

    def _L0_attn_ref(x, W_qkv, W_out):
        import jax, jax.numpy as jnp
        import numpy as np
        B, L, E, H = (2, 512, 128, 16)
        D = E // H
        CHUNK = 32

        def _linear_attention(x, W_qkv, W_out):
            Bz, Lz, Ez = x.shape
            scale = D ** (-0.5)
            qkv = x @ W_qkv.T
            qkv = qkv.reshape(Bz, Lz, 3, H, D).transpose(2, 0, 3, 1, 4)
            q, k, v = (qkv[0], qkv[1], qkv[2])
            q = (jax.nn.elu(q) + 1.0) * scale
            k = jax.nn.elu(k) + 1.0
            nc = Lz // CHUNK

            def to_chunks(t):
                return t.reshape(Bz, H, nc, CHUNK, D).transpose(2, 0, 1, 3, 4)
            qc, kc, vc = (to_chunks(q), to_chunks(k), to_chunks(v))
            causal = jnp.tril(jnp.ones((CHUNK, CHUNK), dtype=x.dtype))

            def step(carry, inp):
                S, Z = carry
                qi, ki, vi = inp
                attn = jnp.einsum('bhld,bhmd->bhlm', qi, ki) * causal
                num = jnp.einsum('bhlm,bhme->bhle', attn, vi) + jnp.einsum('bhld,bhde->bhle', qi, S)
                den = attn.sum(-1) + jnp.einsum('bhld,bhd->bhl', qi, Z)
                S = S + jnp.einsum('bhmd,bhme->bhde', ki, vi)
                Z = Z + ki.sum(axis=2)
                return ((S, Z), (num, den))
            S0 = jnp.zeros((Bz, H, D, D), dtype=x.dtype)
            Z0 = jnp.zeros((Bz, H, D), dtype=x.dtype)
            _, (num, den) = jax.lax.scan(step, (S0, Z0), (qc, kc, vc))
            num = num.transpose(1, 2, 0, 3, 4).reshape(Bz, H, Lz, D)
            den = den.transpose(1, 2, 0, 3).reshape(Bz, H, Lz)
            den = jnp.maximum(den, 1e-06)
            out = num / den[..., None]
            out = out.transpose(0, 2, 1, 3).reshape(Bz, Lz, Ez)
            return out @ W_out.T
        return _linear_attention(x, W_qkv, W_out)

    def _L0_ffn_ref(hidden_states, gate_w, gate_bias, Wg, Wu, Wd, Sg, Su, Sd):
        import jax, jax.numpy as jnp
        import numpy as np
        H = 128
        I = 88
        E = 64
        TOP_K = 8
        NG = 8
        TOPK_GROUP = 4
        N_SHARED = 2
        ROUTED_SCALE = 2.5
        S_I = I * N_SHARED

        def _route(x, gate_w, gate_bias):
            T = x.shape[0]
            logits = x @ gate_w.T
            scores = jax.nn.sigmoid(logits)
            scores_for_choice = scores + gate_bias[None, :]
            grp = scores_for_choice.reshape(T, NG, E // NG)
            group_scores = jnp.sum(jax.lax.top_k(grp, 2)[0], axis=-1)
            _, gidx = jax.lax.top_k(group_scores, TOPK_GROUP)
            gmask = jnp.zeros((T, NG), dtype=scores.dtype).at[jnp.arange(T)[:, None], gidx].set(1.0)
            emask = jnp.repeat(gmask, E // NG, axis=1)
            masked = jnp.where(emask > 0, scores_for_choice, 0.0)
            _, topk_idx = jax.lax.top_k(masked, TOP_K)
            topk_w = jnp.take_along_axis(scores, topk_idx, axis=1)
            topk_w = topk_w / (jnp.sum(topk_w, axis=-1, keepdims=True) + 1e-20)
            topk_w = topk_w * ROUTED_SCALE
            rw = jnp.zeros((T, E), dtype=scores.dtype).at[jnp.arange(T)[:, None], topk_idx].add(topk_w)
            return rw

        def _mlp(x, gw, uw, dw):
            return jax.nn.silu(x @ gw.T) * (x @ uw.T) @ dw.T
        B, S, _ = hidden_states.shape
        x = hidden_states.reshape(B * S, H)
        rw = _route(x, gate_w, gate_bias)
        expert_out = jax.vmap(lambda gw_, uw_, dw_: _mlp(x, gw_, uw_, dw_))(Wg, Wu, Wd)
        routed = jnp.einsum('eth,te->th', expert_out, rw)
        shared = _mlp(x, Sg, Su, Sd)
        out = (routed + shared).reshape(B, S, H)
        return out
    x = L0_attn_x
    x = _layernorm(x + _L0_attn_ref(x, L0_attn_W_qkv, L0_attn_W_out), axis=-1)
    x = _layernorm(x + _L0_ffn_ref(x, L0_ffn_gate_w, L0_ffn_gate_bias, L0_ffn_Wg, L0_ffn_Wu, L0_ffn_Wd, L0_ffn_Sg, L0_ffn_Su, L0_ffn_Sd), axis=-1)
    return x

_drawn_inputs = setup_inputs


def setup_inputs(seed=0):
    import zlib

    import numpy as np

    out = dict(_drawn_inputs(seed))
    spreads = {}
    factors = {'L0_attn_W_qkv': 8.0,
     'L0_attn_W_out': 8.0,
     'L0_ffn_gate_w': 8.0,
     'L0_ffn_gate_bias': 8.0,
     'L0_ffn_Wg': 8.0,
     'L0_ffn_Wu': 8.0,
     'L0_ffn_Wd': 8.0,
     'L0_ffn_Sg': 8.0,
     'L0_ffn_Su': 8.0,
     'L0_ffn_Sd': 8.0}
    for name, (base, spread) in spreads.items():
        noise = np.random.default_rng([zlib.crc32(name.encode()), seed]).standard_normal(out[name].shape)
        drawn = base * np.exp(spread * noise) if base else spread * noise
        out[name] = jnp.asarray(drawn.astype(out[name].dtype))
    for name, factor in factors.items():
        out[name] = (out[name] * factor).astype(out[name].dtype)
    return out
```

```python
from contextlib import ExitStack

import concourse.bass as bass
from concourse import mybir

TOK, E = 2048, 128
BATCH, SEQ = 4, 512
HEADS, HD = 16, 8
P = 128
NT = TOK // P
TPB = SEQ // P
NE, INTER = 64, 88
SHARED = 2 * INTER
GROUPS, TOPK, TOPG = 8, 8, 4
GE = NE // GROUPS
RSCALE = 2.5
SC = -(-SHARED // P)
RC = NE * INTER // P
NCH = SC + RC
QB = TOK // 512
HA = HD + 1
GH = 4
CW = 4 * P

C_CAUSAL = 0
C_HMASK = C_CAUSAL + P
C_BMASK = C_HMASK + GH
C_TRI = C_BMASK + HEADS * HA
C_IDENT = C_TRI + GROUPS * GROUPS
C_END = C_IDENT + P


def build(nc, x_tok, x_t, w_qkv, w_out, gate_w, gate_bias, w_chunks, consts, out):
    f32 = mybir.dt.float32
    f32r = mybir.dt.float32r
    ALU = mybir.AluOpType
    ACT = mybir.ActivationFunctionType
    AX = mybir.AxisListType
    ds = bass.ds

    ctx = ExitStack()
    with ctx:
        def sb(name, shape, dt=f32):
            return ctx.enter_context(nc.sbuf_tensor(name, shape, dt))

        def sem(name):
            return ctx.enter_context(nc.semaphore(name))

        xtok = sb("xtok", [P, NT, E])
        xt = sb("xt", [P, 4, P])
        wqkv = sb("wqkv", [P, 3 * E])
        wo = sb("wo", [P, E])
        gw = sb("gw", [P, NE])
        bias = sb("bias", [P, NE])
        cst = sb("cst", [P, C_END])
        causal = cst[:, C_CAUSAL:C_CAUSAL + P]
        hmask = cst[:, C_HMASK:C_HMASK + GH]
        bmask = cst[:, C_BMASK:C_BMASK + HEADS * HA]
        tri = cst[:, C_TRI:C_TRI + GROUPS * GROUPS]
        ident = cst[:, C_IDENT:C_IDENT + P]
        neg = sb("neg", [P, 4, 3 * P])
        fea = sb("fea", [P, 4, 3 * P])
        vaug = sb("vaug", [P, 4, HEADS, HA])
        qm = sb("qm", [P, 4, GH, P])
        am = sb("am", [P, 2, HEADS, P])
        sm = sb("sm", [P, 4, HEADS * HA])
        den = sb("den", [P, 2, HEADS])
        rden = sb("rden", [P, 2, HEADS])
        ao = sb("ao", [P, 2, E])
        aot = sb("aot", [P, 2, E])
        xa = sb("xa", [P, TPB, E])
        bns = sb("bns", [P, TPB, 6])
        st = sb("st", [P, TPB, 5])
        mean = sb("mean", [P, TPB])
        vare = sb("vare", [P, TPB])
        std = sb("std", [P, TPB])
        rstd = sb("rstd", [P, TPB])
        x1s = sb("x1s", [P, TPB, E])
        x1ts = sb("x1ts", [P, TPB * P])
        x1 = sb("x1", [P, NT, E])
        x1th = sb("x1th", [P, TOK], f32r)
        x1tl = sb("x1tl", [P, TOK], f32r)
        lg = sb("lg", [P, NT, NE])
        sc = sb("sc", [P, NT, NE])
        sfc = sb("sfc", [P, NT * GROUPS, GE])
        ta = sb("ta", [P, NT * GROUPS, 4])
        tb = sb("tb", [P, NT * GROUPS, 4])
        tc = sb("tc", [P, NT * GROUPS, 2])
        td = sb("td", [P, NT * GROUPS, 2])
        te = sb("te", [P, NT * GROUPS, 2])
        tf = sb("tf", [P, NT * GROUPS, 1])
        gs = sb("gs", [P, NT, GROUPS])
        c1 = sb("c1", [P, NT, GROUPS * GROUPS])
        c2 = sb("c2", [P, NT, GROUPS * GROUPS])
        rank = sb("rank", [P, NT * GROUPS])
        top = sb("top", [P, NT, TOPK])
        wsum = sb("wsum", [P, NT])
        rw2 = sb("rw2", [P, NT, 2, NE])
        rt = sb("rt", [P, TOK], f32r)
        raw = sb("raw", [P, 2, CW])
        wh = sb("wh", [P, 2, CW], f32r)
        wl = sb("wl", [P, 2, 3 * P], f32r)
        sg = sb("sg", [P, 4, 512])
        ug = sb("ug", [P, 4, 512])
        hh = sb("hh", [P, 4, 512])
        hhi = sb("hhi", [P, 4, 512], f32r)
        hlo = sb("hlo", [P, 4, 512], f32r)
        osb = sb("osb", [P, QB, 512])
        z = sb("z", [P, NT, E])
        bns2 = sb("bns2", [P, NT, 6])
        mv2 = sb("mv2", [P, NT, 2])
        vare2 = sb("vare2", [P, NT])
        std2 = sb("std2", [P, NT])
        rstd2 = sb("rstd2", [P, NT])
        yo = xtok

        bank = [ctx.enter_context(nc.psum_tensor(f"bank{i}", [P, 512], f32)) for i in range(8)]
        pj, ob, sbk, tbk = bank[0], bank[1], bank[2], bank[3]
        att = bank[4:8]
        ou = bank[0:4]
        gbk = [bank[4], bank[7]]
        ubk, rbk = bank[5], bank[6]

        s_cst = sem("s_cst")
        s_xtok = sem("s_xtok")
        s_xt = [sem(f"s_xt{i}") for i in range(4)]
        s_ones = sem("s_ones")
        s_proj = sem("s_proj")
        s_min = sem("s_min")
        s_exp = sem("s_exp")
        s_elu = sem("s_elu")
        s_vev = sem("s_vev")
        s_qm = sem("s_qm")
        s_att = sem("s_att")
        s_mask = sem("s_mask")
        s_o = sem("s_o")
        s_st = sem("s_st")
        s_sm = sem("s_sm")
        s_den = sem("s_den")
        s_rden = sem("s_rden")
        s_ao = sem("s_ao")
        s_aot = sem("s_aot")
        s_aote = sem("s_aote")
        s_y = sem("s_y")
        s_xa = sem("s_xa")
        s_bn = sem("s_bn")
        s_mv = sem("s_mv")
        s_vare = sem("s_vare")
        s_std = sem("s_std")
        s_rstd = sem("s_rstd")
        s_x1 = sem("s_x1")
        s_x1c = sem("s_x1c")
        s_x1t = sem("s_x1t")
        s_x1te = sem("s_x1te")
        s_x1h = sem("s_x1h")
        s_x1l = sem("s_x1l")
        s_lg = sem("s_lg")
        s_lge = sem("s_lge")
        s_sig = sem("s_sig")
        s_rch = sem("s_rch")
        s_rw = sem("s_rw")
        s_rtt = sem("s_rtt")
        s_rte = sem("s_rte")
        s_raw = [sem(f"s_raw{i}") for i in range(2)]
        s_wh = sem("s_wh")
        s_wl = sem("s_wl")
        s_g = sem("s_g")
        s_u = sem("s_u")
        s_r = sem("s_r")
        s_silu = sem("s_silu")
        s_ug = sem("s_ug")
        s_h = sem("s_h")
        s_hhi = sem("s_hhi")
        s_hlo = sem("s_hlo")
        s_d = sem("s_d")
        s_osb = sem("s_osb")
        s_ot = sem("s_ot")
        s_z = sem("s_z")
        s_bn2 = sem("s_bn2")
        s_mv2 = sem("s_mv2")
        s_va2 = sem("s_va2")
        s_sd2 = sem("s_sd2")
        s_rs2 = sem("s_rs2")
        s_yo = sem("s_yo")
        s_out = sem("s_out")

        block = ctx.enter_context(nc.Block())

        @block.sync
        def _(sp):
            def load_x(t, b, c):
                sp.dma_start(xt[:, c, :], x_t[:, ds(t * P, P)]).then_inc(s_xt[c], 16)

            for c in range(4):
                load_x(c, 0, c)
                if c == 0:
                    sp.dma_start(wqkv[:, :], w_qkv).then_inc(s_cst, 16)
                    sp.dma_start(cst[:, :], consts).then_inc(s_cst, 16)
            sp.dma_start(wo[:, :], w_out).then_inc(s_cst, 16)
            sp.dma_start(gw[:, :], gate_w).then_inc(s_cst, 16)
            sp.dma_start(bias[:, :], gate_bias).then_inc(s_cst, 16)
            sp.dma_start(xtok[:, :, :], x_tok).then_inc(s_xtok, 16)
            for ci in range(2):
                sp.dma_start(raw[:, ci, :], w_chunks[ci]).then_inc(s_raw[ci], 16)
            with sp.Fori(1, BATCH) as b:
                for c in range(4):
                    sp.wait_ge(s_proj, 4 * b + c - 3)
                    load_x(4 * b + c, b, c)
            with sp.Fori(1, NCH // 2) as i:
                for k in range(2):
                    sp.wait_ge(s_wh, 2 * i + k - 1)
                    sp.wait_ge(s_wl, 2 * i + k - 1)
                    sp.dma_start(raw[:, k, :], w_chunks[ds(2 * i + k, 1)].rearrange("a p n -> p (a n)"))\
                      .then_inc(s_raw[k], 16)
            for n in range(QB):
                sp.wait_ge(s_yo, 4 * (n + 1))
                sp.dma_start(out[:, 4 * n:4 * n + 4, :], yo[:, 4 * n:4 * n + 4, :]).then_inc(s_out, 16)
            sp.wait_ge(s_out, 16 * QB)

        @block.gpsimd
        def _(pool):
            for c in range(4):
                pool.memset(vaug[:, c, :, HD:HA], 1.0).then_inc(s_ones, 1)
            pool.sem_inc(s_x1l, 1)
            pool.wait_ge(s_cst, 80)

            def by_head(t, c):
                pool.wait_ge(s_elu, t + 1)
                nc.gpsimd.tensor_tensor(qm[:, c], fea[:, c, 0:P].unsqueeze(1).to_broadcast([P, GH, P]),
                                        hmask.unsqueeze(2).to_broadcast([P, GH, P]), ALU.mult)\
                    .then_inc(s_qm, 1)

            def finish(b):
                pool.wait_ge(s_x1, 4 * b + 4)
                nc.gpsimd.tensor_copy(x1[:, ds(4 * b, 4), :], x1s[:, :, :]).then_inc(s_x1c, 1)
                pool.wait_ge(s_x1te, b + 1)
                pool.wait_ge(s_x1h, b + 1)
                nc.gpsimd.tensor_tensor(x1tl[:, ds(512 * b, 512)], x1ts[:, :],
                                        x1th[:, ds(512 * b, 512)].bitcast(f32), ALU.subtract)\
                    .then_inc(s_x1l, 1)

            def batch(b, first, last):
                for c in range(4):
                    if not (last and c >= 2):
                        by_head(4 * b + c + 2, (c + 2) % 4)
                    if c == 1 and not first:
                        finish(b - 1)

            by_head(0, 0)
            by_head(1, 1)
            batch(0, True, False)
            with pool.Fori(1, BATCH - 1) as b:
                batch(b, False, False)
            batch(BATCH - 1, False, True)
            finish(BATCH - 1)

            def split_weights(ci, k, i):
                pool.wait_ge(s_wh, ci + 1)
                nc.gpsimd.tensor_tensor(wl[:, k, :], raw[:, k, 0:3 * P], wh[:, k, 0:3 * P].bitcast(f32),
                                        ALU.subtract).then_inc(s_wl, 1)

            def chunk(ci, k, last):
                for n in range(QB):
                    pool.wait_ge(s_hhi, 4 * ci + n + 1)
                    nc.gpsimd.tensor_tensor(hlo[:, n, :], hh[:, n, :], hhi[:, n, :].bitcast(f32),
                                            ALU.subtract).then_inc(s_hlo, 1)
                    if n == 2 and not last:
                        split_weights(ci + 1, 1 - k, 0)

            split_weights(0, 0, 0)
            for ci in range(SC):
                chunk(ci, ci % 2, False)
            with pool.Fori(1, NCH // 2 - 1) as i:
                for k in range(2):
                    chunk(2 * i + k, k, False)
            chunk(NCH - 2, 0, False)
            chunk(NCH - 1, 1, True)

        @block.scalar
        def _(act):
            act.wait_ge(s_ones, 4)

            def exps(t, c):
                act.wait_ge(s_min, t + 1)
                nc.scalar.activation(neg[:, c, :], neg[:, c, :], ACT.Exp).then_inc(s_exp, 1)
                act.wait_ge(s_elu, t + 1)
                nc.scalar.activation(vaug[:, c, :, 0:HD],
                                     pj[:, 3 * P:4 * P].rearrange("p (h d) -> p h d", h=HEADS), ACT.Copy)\
                    .then_inc(s_vev, 1)

            def out_transpose(t, k):
                act.wait_ge(s_aot, t + 1)
                nc.scalar.activation(aot[:, k, :], tbk[:, 0:P], ACT.Copy).then_inc(s_aote, 1)

            def deviation(b):
                act.wait_ge(s_vare, b + 1)
                nc.scalar.activation(std[:, :], vare[:, :], ACT.Sqrt).then_inc(s_std, 1)

            def finish(b):
                act.wait_ge(s_x1t, b + 1)
                act.wait_ge(s_x1l, b + 1)
                nc.scalar.activation(x1ts[:, :], tbk[:, :], ACT.Copy).then_inc(s_x1te, 1)
                nc.scalar.activation(x1th[:, ds(512 * b, 512)], tbk[:, :], ACT.Copy).then_inc(s_x1h, 1)
                act.wait_ge(s_lg, b + 1)
                nc.scalar.activation(lg[:, ds(4 * b, 4), :],
                                     tbk[:, 0:4 * NE].rearrange("p (c e) -> p c e", c=4), ACT.Copy)\
                    .then_inc(s_lge, 1)

            def batch(b, first, last):
                for c in range(4):
                    t = 4 * b + c
                    if not (last and c >= 2):
                        exps(t + 2, (c + 2) % 4)
                    if not (first and c == 0):
                        out_transpose(t - 1, (c + 1) % 2)
                    if c == 0 and not first:
                        deviation(b - 1)
                    if c == 1 and not first:
                        finish(b - 1)

            exps(0, 0)
            exps(1, 1)
            batch(0, True, False)
            with act.Fori(1, BATCH - 1) as b:
                batch(b, False, False)
            batch(BATCH - 1, False, True)
            out_transpose(NT - 1, 1)
            deviation(BATCH - 1)
            finish(BATCH - 1)
            act.wait_ge(s_lge, BATCH)
            nc.scalar.activation(sc[:, :, :], lg[:, :, :], ACT.Sigmoid).then_inc(s_sig, 1)

            def split_weights(ci, k, loaded):
                act.wait_ge(s_raw[k], loaded)
                nc.scalar.activation(wh[:, k, :], raw[:, k, :], ACT.Copy).then_inc(s_wh, 1)

            def upper(u, n):
                act.wait_ge(s_h, u + 1)
                nc.scalar.activation(hhi[:, n, :], hh[:, n, :], ACT.Copy).then_inc(s_hhi, 1)

            def chunk(ci, k, i, first, last):
                for n in range(QB):
                    u = 4 * ci + n
                    act.wait_ge(s_g, u + 1)
                    nc.scalar.activation(sg[:, n, :], gbk[n % 2][:, :], ACT.Silu).then_inc(s_silu, 1)
                    if not (first and n == 0):
                        upper(u - 1, (n + 3) % 4)
                    if n == 2 and not last:
                        if not first:
                            act.wait_ge(s_d, 4 * ci)
                        split_weights(ci + 1, 1 - k, 16 * (i + 1) if k == 0 else 16 * (i + 2))

            split_weights(0, 0, 16)
            chunk(0, 0, 0, True, False)
            chunk(1, 1, 0, False, False)
            for n in range(QB):
                act.wait_ge(s_rtt, n + 1)
                nc.scalar.activation(rt[:, 512 * n:512 * n + 512], rbk[:, :], ACT.Copy).then_inc(s_rte, 1)
            with act.Fori(1, NCH // 2 - 1) as i:
                for k in range(2):
                    chunk(2 * i + k, k, i, False, False)
            chunk(NCH - 2, 0, NCH // 2 - 1, False, False)
            chunk(NCH - 1, 1, NCH // 2 - 1, False, True)
            upper(4 * NCH - 1, 3)
            for n in range(QB):
                act.wait_ge(s_d, 4 * NCH - 3 + n)
                nc.scalar.activation(osb[:, n, :], ou[n][:, :], ACT.Copy).then_inc(s_osb, 1)
            for n in range(QB):
                act.wait_ge(s_va2, n + 1)
                nc.scalar.activation(std2[:, 4 * n:4 * n + 4], vare2[:, 4 * n:4 * n + 4], ACT.Sqrt)\
                    .then_inc(s_sd2, 1)

        @block.vector
        def _(dve):
            V = nc.vector
            dve.wait_ge(s_cst, 80)

            def elu(t, c):
                dve.wait_ge(s_proj, t + 1)
                V.tensor_scalar(neg[:, c, :], pj[:, 0:3 * P], 0.0, None, ALU.min).then_inc(s_min, 1)
                dve.wait_ge(s_exp, t + 1)
                V.scalar_tensor_tensor(fea[:, c, :], pj[:, 0:3 * P], 0.0, neg[:, c, :], ALU.max, ALU.add)\
                    .then_inc(s_elu, 1)

            def mask(t, k):
                for g in range(4):
                    dve.wait_ge(s_att, 4 * t + g + 1)
                    V.tensor_tensor(am[:, k, GH * g:GH * g + GH, :],
                                    att[g][:, :].rearrange("p (h l) -> p h l", h=GH),
                                    causal.unsqueeze(1).to_broadcast([P, GH, P]), ALU.mult)\
                        .then_inc(s_mask, 1)

            def state(b, c):
                dve.wait_ge(s_st, 3 * b + c + 1)
                V.tensor_tensor(sm[:, c, :], sbk[:, 0:HEADS * HA], bmask, ALU.mult).then_inc(s_sm, 1)

            def divide(t, k):
                dve.wait_ge(s_o, t + 1)
                o = ob[:, 0:HEADS * HA].rearrange("p (h a) -> p h a", h=HEADS)
                V.tensor_scalar(den[:, k, :].unsqueeze(2), o[:, :, HD:HA], 1e-6, None, ALU.max).then_inc(s_den, 1)
                dve.wait_ge(s_den, t + 1)
                V.reciprocal(rden[:, k, :], den[:, k, :]).then_inc(s_rden, 1)
                dve.wait_ge(s_rden, t + 1)
                V.tensor_tensor(ao[:, k, :].rearrange("p (h d) -> p h d", h=HEADS), o[:, :, 0:HD],
                                rden[:, k, :].unsqueeze(2).to_broadcast([P, HEADS, HD]), ALU.mult)\
                    .then_inc(s_ao, 1)

            def residual(t, c):
                dve.wait_ge(s_y, t + 1)
                V.tensor_tensor(xa[:, c, :], tbk[:, P:2 * P], xtok[:, ds(t, 1), :].rearrange("p a e -> p (a e)"),
                                ALU.add).then_inc(s_xa, 1)
                dve.wait_ge(s_xa, t + 1)
                V.bn_stats(bns[:, c, :], xa[:, c, :]).then_inc(s_bn, 1)

            def finish_a(b):
                half = E // 2
                dve.wait_ge(s_bn, 4 * b + 4)
                V.tensor_tensor(st[:, :, 0:1], bns[:, :, 1:2], bns[:, :, 4:5], ALU.add).then_inc(s_mv, 1)
                V.tensor_tensor(st[:, :, 1:2], bns[:, :, 1:2], bns[:, :, 4:5], ALU.subtract).then_inc(s_mv, 1)
                V.tensor_tensor(st[:, :, 2:3], bns[:, :, 2:3], bns[:, :, 5:6], ALU.add).then_inc(s_mv, 1)
                dve.wait_ge(s_mv, 6 * b + 3)
                V.tensor_scalar(mean[:, :].unsqueeze(2), st[:, :, 0:1], 0.5, None, ALU.mult).then_inc(s_mv, 1)
                V.tensor_tensor(st[:, :, 3:4], st[:, :, 1:2], st[:, :, 1:2], ALU.mult).then_inc(s_mv, 1)
                V.tensor_scalar(st[:, :, 4:5], st[:, :, 2:3], 0.5 / half, 1e-5, ALU.mult, ALU.add).then_inc(s_mv, 1)
                dve.wait_ge(s_mv, 6 * b + 6)
                V.scalar_tensor_tensor(vare[:, :].unsqueeze(2), st[:, :, 3:4], 0.25, st[:, :, 4:5],
                                       ALU.mult, ALU.add).then_inc(s_vare, 1)

            def finish_b(b):
                dve.wait_ge(s_std, b + 1)
                V.reciprocal(rstd[:, :], std[:, :]).then_inc(s_rstd, 1)
                dve.wait_ge(s_rstd, b + 1)
                dve.wait_ge(s_x1l, b + 1)
                for c in range(4):
                    V.tensor_scalar(x1s[:, c, :], xa[:, c, :], mean[:, c:c + 1], rstd[:, c:c + 1],
                                    ALU.subtract, ALU.mult).then_inc(s_x1, 1)

            def batch(b, first, last):
                for c in range(4):
                    t = 4 * b + c
                    if not (last and c >= 2):
                        elu(t + 2, (c + 2) % 4)
                    if not (last and c == 3):
                        mask(t + 1, (c + 1) % 2)
                    if c == 0 and not first:
                        residual(t - 1, 3)
                        finish_a(b - 1)
                        finish_b(b - 1)
                    elif c:
                        residual(t - 1, c - 1)
                    divide(t, c % 2)
                    if c < 3:
                        state(b, c)

            elu(0, 0)
            elu(1, 1)
            dve.wait_ge(s_xtok, 16)
            mask(0, 0)
            batch(0, True, False)
            with dve.Fori(1, BATCH - 1) as b:
                batch(b, False, False)
            batch(BATCH - 1, False, True)
            residual(NT - 1, 3)
            finish_a(BATCH - 1)
            finish_b(BATCH - 1)

            steps = [0]

            def step(ins):
                steps[0] += 1
                ins.then_inc(s_rch, 1)

            def after():
                dve.wait_ge(s_rch, steps[0])

            def shared_unit(u):
                n = u % 4
                dve.wait_ge(s_silu, u + 1)
                dve.wait_ge(s_u, u + 1)
                V.tensor_tensor(hh[:, n, :], ubk[:, :], sg[:, n, :], ALU.mult).then_inc(s_h, 1)

            dve.wait_ge(s_sig, 1)
            sview = sfc[:, :, :].rearrange("p (t g) e -> p t (g e)", t=NT)
            step(V.tensor_tensor(sview, sc[:, :, :], bias[:, :].unsqueeze(1).to_broadcast([P, NT, NE]), ALU.add))
            shared_unit(0)
            after()
            step(V.tensor_tensor(ta[:, :, :], sfc[:, :, 0:4], sfc[:, :, 4:8], ALU.max))
            step(V.tensor_tensor(tb[:, :, :], sfc[:, :, 0:4], sfc[:, :, 4:8], ALU.min))
            shared_unit(1)
            after()
            step(V.tensor_tensor(tc[:, :, :], ta[:, :, 0:2], ta[:, :, 2:4], ALU.max))
            step(V.tensor_tensor(td[:, :, :], ta[:, :, 0:2], ta[:, :, 2:4], ALU.min))
            step(V.tensor_tensor(te[:, :, :], tb[:, :, 0:2], tb[:, :, 2:4], ALU.max))
            after()
            step(V.tensor_tensor(te[:, :, :], te[:, :, :], td[:, :, :], ALU.max))
            after()
            step(V.tensor_tensor(ta[:, :, 0:1], tc[:, :, 0:1], tc[:, :, 1:2], ALU.max))
            step(V.tensor_tensor(tb[:, :, 0:1], tc[:, :, 0:1], tc[:, :, 1:2], ALU.min))
            step(V.tensor_tensor(tf[:, :, :], te[:, :, 0:1], te[:, :, 1:2], ALU.max))
            after()
            step(V.tensor_tensor(tb[:, :, 0:1], tb[:, :, 0:1], tf[:, :, :], ALU.max))
            after()
            gsv = gs[:, :, :].rearrange("p t g -> p (t g)")
            step(V.tensor_tensor(gsv.unsqueeze(2), ta[:, :, 0:1], tb[:, :, 0:1], ALU.add))
            shared_unit(2)
            c1v = c1[:, :, :].rearrange("p t (i j) -> p t i j", i=GROUPS)
            c2v = c2[:, :, :].rearrange("p t (i j) -> p t i j", i=GROUPS)
            gj = gs[:, :, :].unsqueeze(2).to_broadcast([P, NT, GROUPS, GROUPS])
            gi = gs[:, :, :].unsqueeze(3).to_broadcast([P, NT, GROUPS, GROUPS])
            after()
            step(V.tensor_tensor(c1v, gj, gi, ALU.is_equal))
            step(V.tensor_tensor(c2v, gj, gi, ALU.is_gt))
            shared_unit(3)
            after()
            step(V.tensor_tensor(c1[:, :, :], c1[:, :, :],
                                 tri.unsqueeze(1).to_broadcast([P, NT, GROUPS * GROUPS]), ALU.mult))
            after()
            step(V.tensor_tensor(c1[:, :, :], c1[:, :, :], c2[:, :, :], ALU.add))
            shared_unit(4)
            after()
            step(V.tensor_reduce(rank[:, :], c1[:, :, :].rearrange("p t (i j) -> p (t i) j", i=GROUPS),
                                 AX.X, ALU.add))
            after()
            step(V.tensor_scalar(rank[:, :], rank[:, :], float(TOPG), None, ALU.is_lt))
            after()
            step(V.tensor_tensor(sfc[:, :, :], sfc[:, :, :],
                                 rank[:, :].unsqueeze(2).to_broadcast([P, NT * GROUPS, GE]), ALU.mult))
            shared_unit(5)
            after()
            step(V.tensor_scalar(sfc[:, :, :], sfc[:, :, :], 0.0, None, ALU.add))
            after()
            for t in range(NT):
                step(V.max(top[:, t, :], sview[:, t, :]))
            shared_unit(6)
            after()
            for t in range(NT):
                step(V.match_replace(lg[:, t, :], top[:, t, :], sview[:, t, :], -3.0e38))
            shared_unit(7)
            after()
            step(V.tensor_tensor(lg[:, :, :], lg[:, :, :], sview, ALU.not_equal))
            after()
            step(V.tensor_tensor(sc[:, :, :], sc[:, :, :], lg[:, :, :], ALU.mult))
            after()
            step(V.tensor_reduce(wsum[:, :], sc[:, :, :], AX.X, ALU.add))
            after()
            step(V.tensor_scalar(wsum[:, :], wsum[:, :], 1e-20, None, ALU.add))
            after()
            step(V.reciprocal(wsum[:, :], wsum[:, :]))
            after()
            step(V.tensor_tensor(sc[:, :, :], sc[:, :, :], wsum[:, :].unsqueeze(2).to_broadcast([P, NT, NE]),
                                 ALU.mult))
            after()
            step(V.tensor_scalar(sc[:, :, :], sc[:, :, :], RSCALE, None, ALU.mult))
            after()
            step(V.tensor_scalar(rw2[:, :, 0, :].bitcast(f32r), sc[:, :, :], 1.0, None, ALU.mult))
            after()
            V.tensor_tensor(rw2[:, :, 1, :], sc[:, :, :], rw2[:, :, 0, :], ALU.subtract).then_inc(s_rw, 1)

            def chunk(ci):
                for n in range(QB):
                    u = 4 * ci + n
                    r = u - 4 * SC
                    dve.wait_ge(s_silu, u + 1)
                    dve.wait_ge(s_u, u + 1)
                    V.tensor_tensor(ug[:, n, :], ubk[:, :], sg[:, n, :], ALU.mult).then_inc(s_ug, 1)
                    dve.wait_ge(s_ug, r + 1)
                    dve.wait_ge(s_r, r + 1)
                    V.tensor_tensor(hh[:, n, :], rbk[:, :], ug[:, n, :], ALU.mult).then_inc(s_h, 1)

            with dve.Fori(1, NCH // 2) as i:
                for k in range(2):
                    chunk(2 * i + k)

            for n in range(QB):
                dve.wait_ge(s_ot, n + 1)
                q = slice(4 * n, 4 * n + 4)
                V.tensor_tensor(z[:, q, :], bank[4 + n][:, :].rearrange("p (c e) -> p c e", c=4), x1[:, q, :],
                                ALU.add).then_inc(s_z, 1)
                dve.wait_ge(s_z, n + 1)
                for t in range(4 * n, 4 * n + 4):
                    V.bn_stats(bns2[:, t, :], z[:, t, :]).then_inc(s_bn2, 1)
                for t in range(4 * n, 4 * n + 4):
                    dve.wait_ge(s_bn2, t + 1)
                    V.bn_aggr(mv2[:, t, :], bns2[:, t, :]).then_inc(s_mv2, 1)
                dve.wait_ge(s_mv2, 4 * n + 4)
                V.tensor_scalar(vare2[:, q].unsqueeze(2), mv2[:, q, 1:2], 1e-5, None, ALU.add).then_inc(s_va2, 1)
            for n in range(QB):
                q = slice(4 * n, 4 * n + 4)
                dve.wait_ge(s_sd2, n + 1)
                V.reciprocal(rstd2[:, q], std2[:, q]).then_inc(s_rs2, 1)
                dve.wait_ge(s_rs2, n + 1)
                for t in range(4 * n, 4 * n + 4):
                    V.tensor_scalar(yo[:, t, :], z[:, t, :], mv2[:, t, 0:1], rstd2[:, t:t + 1],
                                    ALU.subtract, ALU.mult).then_inc(s_yo, 1)

        @block.tensor
        def _(pe):
            mm = nc.tensor.matmul

            def project(t, c, nth, first):
                pe.wait_ge(s_xt[c], 16 * nth)
                if not first:
                    pe.wait_ge(s_elu, t)
                    pe.wait_ge(s_vev, t)
                mm(pj[:, 0:P], wqkv[:, 0:E], xt[:, c, :], start=True, stop=True)
                mm(pj[:, P:2 * P], wqkv[:, E:2 * E], xt[:, c, :], start=True, stop=True)
                mm(pj[:, 2 * P:4 * P], xt[:, c, :], wqkv[:, E:3 * E], start=True, stop=True).then_inc(s_proj, 1)

            def scores(t, c, first):
                pe.wait_ge(s_qm, t + 1)
                pe.wait_ge(s_elu, t + 1)
                for g in range(4):
                    if not first:
                        pe.wait_ge(s_mask, 4 * t + g - 3)
                    rows = slice(32 * g, 32 * g + 32)
                    mm(att[g][:, :], fea[rows, c, P:2 * P], qm[rows, c].rearrange("p h l -> p (h l)"),
                       start=True, stop=True).then_inc(s_att, 1)

            def sums(b, c, first):
                t = 4 * b + c
                pe.wait_ge(s_mask, 4 * t + 4)
                pe.wait_ge(s_vev, t + 1)
                if not first:
                    pe.wait_ge(s_ao, t)
                if c:
                    pe.wait_ge(s_sm, 3 * b + c)
                    mm(ob[:, 0:HEADS * HA], fea[:, c, 0:P], sm[:, c - 1, :], start=True, stop=False,
                       skip_group_check=True)
                for h in range(HEADS):
                    last = mm(ob[:, HA * h:HA * h + HA], am[:, c % 2, h, :], vaug[:, c, h, :],
                              start=(c == 0 and h == 0), stop=(h == HEADS - 1), skip_group_check=True)
                last.then_inc(s_o, 1)
                if c < 3:
                    if c == 0 and not first:
                        pe.wait_ge(s_sm, 3 * b)
                    elif c:
                        pe.wait_ge(s_sm, 3 * b + c)
                    mm(sbk[:, 0:HEADS * HA], fea[:, c, 2 * P:3 * P],
                       vaug[:, c].rearrange("p h a -> p (h a)"), start=(c == 0), stop=True,
                       skip_group_check=True).then_inc(s_st, 1)

            def output(t, k, first):
                pe.wait_ge(s_ao, t + 1)
                if not first:
                    pe.wait_ge(s_xa, t)
                nc.tensor.transpose(tbk[:, 0:P], ao[:, k, :], ident).then_inc(s_aot, 1)
                pe.wait_ge(s_aote, t + 1)
                mm(tbk[:, P:2 * P], aot[:, k, :], wo[:, :], start=True, stop=True).then_inc(s_y, 1)

            def finish(b):
                pe.wait_ge(s_x1, 4 * b + 4)
                for c in range(4):
                    last = nc.tensor.transpose(tbk[:, P * c:P * c + P], x1s[:, c, :], ident)
                last.then_inc(s_x1t, 1)
                pe.wait_ge(s_x1te, b + 1)
                pe.wait_ge(s_x1h, b + 1)
                for c in range(4):
                    last = mm(tbk[:, NE * c:NE * c + NE], x1ts[:, P * c:P * c + P], gw[:, :], start=True, stop=True)
                last.then_inc(s_lg, 1)

            def batch(b, first, last):
                for c in range(4):
                    t = 4 * b + c
                    if not (last and c >= 2):
                        project(t + 2, (c + 2) % 4, b + 1 + (c >= 2), False)
                    if not (last and c == 3):
                        scores(t + 1, (c + 1) % 4, False)
                    if c == 2 and not first:
                        pe.wait_ge(s_lge, b)
                    if not (first and c == 0):
                        output(t - 1, (c + 1) % 2, first and c == 1)
                    if c == 1 and not first:
                        pe.wait_ge(s_xa, t)
                        finish(b - 1)
                    sums(b, c, first and c == 0)

            pe.wait_ge(s_cst, 80)
            project(0, 0, 1, True)
            project(1, 1, 1, False)
            scores(0, 0, True)
            batch(0, True, False)
            with pe.Fori(1, BATCH - 1) as b:
                batch(b, False, False)
            batch(BATCH - 1, False, True)
            output(NT - 1, 1, False)
            finish(BATCH - 1)

            def product(dst, k, col, hi, lo, start, stop):
                mm(dst, wh[:, k, col:col + P], hi, start=start, stop=False, skip_group_check=True)
                mm(dst, wh[:, k, col:col + P], lo, start=False, stop=False, skip_group_check=True)
                return mm(dst, wl[:, k, col:col + P], hi, start=False, stop=stop, skip_group_check=True)

            def down(u, k, n, start):
                pe.wait_ge(s_hlo, u + 1)
                product(ou[n][:, :], k, 2 * P, hhi[:, n, :], hlo[:, n, :], start, True).then_inc(s_d, 1)

            def chunk(ci, k, routed, first_ever=False, first_routed=False, start_banks=False):
                pe.wait_ge(s_wh, ci + 1)
                pe.wait_ge(s_wl, ci + 1)
                for n in range(QB):
                    u = 4 * ci + n
                    r = u - 4 * SC
                    xs = slice(512 * n, 512 * n + 512)
                    if not (first_ever and n < 2):
                        pe.wait_ge(s_silu, u - 1)
                    product(gbk[n % 2][:, :], k, 0, x1th[:, xs], x1tl[:, xs], True, True).then_inc(s_g, 1)
                    if not routed or (first_routed and n == 0):
                        if not (first_ever and n == 0):
                            pe.wait_ge(s_h, u)
                    else:
                        pe.wait_ge(s_ug, r)
                    product(ubk[:, :], k, P, x1th[:, xs], x1tl[:, xs], True, True).then_inc(s_u, 1)
                    if routed:
                        pe.wait_ge(s_h, u)
                        mm(rbk[:, :], wh[:, k, 3 * P:4 * P], rt[:, xs], start=True, stop=True).then_inc(s_r, 1)
                    if not (first_ever and n < 2):
                        down(u - 2, k if n >= 2 else 1 - k, (n + 2) % 4,
                             first_ever or (start_banks and n < 2))

            pe.wait_ge(s_lge, BATCH)
            pe.wait_ge(s_x1l, BATCH + 1)
            chunk(0, 0, False, first_ever=True)
            chunk(1, 1, False, start_banks=True)
            pe.wait_ge(s_rw, 1)
            for n in range(QB):
                if n:
                    pe.wait_ge(s_rte, n)
                for c in range(4):
                    last = nc.tensor.transpose(rbk[:, P * c:P * c + P],
                                               rw2[:, 4 * n + c].rearrange("p a e -> p (a e)"), ident)
                last.then_inc(s_rtt, 1)
            pe.wait_ge(s_rte, QB)
            chunk(2, 0, True, first_routed=True)
            chunk(3, 1, True)
            with pe.Fori(2, NCH // 2) as i:
                for k in range(2):
                    chunk(2 * i + k, k, True)
            down(4 * NCH - 2, 1, 2, False)
            down(4 * NCH - 1, 1, 3, False)
            for n in range(QB):
                pe.wait_ge(s_osb, n + 1)
                if n == 0:
                    pe.wait_ge(s_h, 4 * NCH)
                for c in range(4):
                    last = nc.tensor.transpose(bank[4 + n][:, P * c:P * c + P], osb[:, n, P * c:P * c + P], ident)
                last.then_inc(s_ot, 1)


def layouts(L0_attn_x, L0_attn_W_qkv, L0_attn_W_out, L0_ffn_gate_w, L0_ffn_gate_bias, L0_ffn_Wg, L0_ffn_Wu,
            L0_ffn_Wd, L0_ffn_Sg, L0_ffn_Su, L0_ffn_Sd):
    import numpy as np

    x = np.asarray(L0_attn_x).reshape(TOK, E)
    chunks = np.zeros((NCH, P, CW), np.float32)

    def rows_to_columns(w, first, count, at):
        full = np.zeros((count * P, E), np.float32)
        full[:w.shape[0]] = w
        chunks[first:first + count, :, at:at + P] = full.reshape(count, P, E).transpose(0, 2, 1)

    rows_to_columns(np.asarray(L0_ffn_Sg), 0, SC, 0)
    rows_to_columns(np.asarray(L0_ffn_Su), 0, SC, P)
    rows_to_columns(np.asarray(L0_ffn_Wg).reshape(NE * INTER, E), SC, RC, 0)
    rows_to_columns(np.asarray(L0_ffn_Wu).reshape(NE * INTER, E), SC, RC, P)
    sd = np.zeros((SC * P, E), np.float32)
    sd[:SHARED] = np.asarray(L0_ffn_Sd).T
    chunks[0:SC, :, 2 * P:3 * P] = sd.reshape(SC, P, E)
    chunks[SC:, :, 2 * P:3 * P] = np.asarray(L0_ffn_Wd).transpose(0, 2, 1).reshape(RC, P, E)
    expert = np.arange(NE * INTER) // INTER
    pick = (np.arange(P)[:, None] % NE == expert[None, :]).astype(np.float32)
    chunks[SC:, :, 3 * P:4 * P] = pick.reshape(P, RC, P).transpose(1, 0, 2)

    cst = np.zeros((P, C_END), np.float32)
    p = np.arange(P)
    scale = float(HD) ** -0.5
    cst[:, C_CAUSAL:C_CAUSAL + P] = p[:, None] <= p[None, :]
    cst[:, C_HMASK:C_HMASK + GH] = (p[:, None] // HD % GH == np.arange(GH)[None, :]) * scale
    cst[:, C_BMASK:C_BMASK + HEADS * HA] = (p[:, None] // HD == np.arange(HEADS * HA)[None, :] // HA) * scale
    g = np.arange(GROUPS)
    cst[:, C_TRI:C_TRI + GROUPS * GROUPS] = (g[None, :] < g[:, None]).reshape(1, -1)
    cst[:, C_IDENT:C_IDENT + P] = p[:, None] == p[None, :]
    return {
        "x_tok": np.ascontiguousarray(x.reshape(NT, P, E).transpose(1, 0, 2)),
        "x_t": np.ascontiguousarray(x.T),
        "w_qkv": np.ascontiguousarray(np.asarray(L0_attn_W_qkv).T),
        "w_out": np.ascontiguousarray(np.asarray(L0_attn_W_out).T),
        "gate_w": np.ascontiguousarray(np.asarray(L0_ffn_gate_w).T),
        "gate_bias": np.ascontiguousarray(np.broadcast_to(np.asarray(L0_ffn_gate_bias)[None, :], (P, NE))),
        "w_chunks": chunks,
        "consts": cst,
    }


def kernel(**inputs):
    import concourse.bacc as _bacc
    from concourse.bass_utils import run_bass_kernel_spmd as _run

    nc = _bacc.Bacc("TRN2", target_bir_lowering=False, num_devices=1)
    arrays, args = {}, []
    for name, a in layouts(**inputs).items():
        arrays[f"in_{name}"] = a
        args.append(nc.dram_tensor(f"in_{name}", a.shape, mybir.dt.from_np(a.dtype), kind="ExternalInput").ap())
    o = nc.dram_tensor("out_x", (BATCH, SEQ, E), mybir.dt.float32, kind="ExternalOutput").ap()
    build(nc, *args, o.rearrange("b (j p) e -> p (b j) e", p=P))
    r = _run(nc, [arrays], core_ids=[0])
    return r.results[0]["out_x"]
```

```python
from contextlib import ExitStack

import concourse.bass as bass
from concourse import mybir

TOK, E = 2048, 128
BATCH, SEQ = 4, 512
HEADS, HD = 16, 8
P = 128
NT = TOK // P
TPB = SEQ // P
NE, INTER = 64, 88
SHARED = 2 * INTER
GROUPS, TOPK, TOPG = 8, 8, 4
GE = NE // GROUPS
RSCALE = 2.5
SC = -(-SHARED // P)
RC = NE * INTER // P
NCH = SC + RC
QB = TOK // 512
HA = HD + 1
HP = HA * HD
THIRDS = ((0, 6), (6, 5), (11, 5))
CW = 4 * P

C_CAUSAL = 0
C_BMASK = C_CAUSAL + P
C_TRI = C_BMASK + HEADS * HA
C_IDENT = C_TRI + GROUPS * GROUPS
C_END = C_IDENT + P


def build(nc, x_tok, x_t, w_qkv, w_out, gate_w, gate_bias, w_chunks, consts, out):
    f32 = mybir.dt.float32
    f32r = mybir.dt.float32r
    ALU = mybir.AluOpType
    ACT = mybir.ActivationFunctionType
    AX = mybir.AxisListType
    ds = bass.ds

    ctx = ExitStack()
    with ctx:
        def sb(name, shape, dt=f32):
            return ctx.enter_context(nc.sbuf_tensor(name, shape, dt))

        def sem(name):
            return ctx.enter_context(nc.semaphore(name))

        xtok = sb("xtok", [P, NT, E])
        xt = sb("xt", [P, 4, P])
        wqkv = sb("wqkv", [P, 3 * E])
        wo = sb("wo", [P, E])
        gw = sb("gw", [P, NE])
        bias = sb("bias", [P, NE])
        cst = sb("cst", [P, C_END])
        causal = cst[:, C_CAUSAL:C_CAUSAL + P]
        bmask = cst[:, C_BMASK:C_BMASK + HEADS * HA]
        tri = cst[:, C_TRI:C_TRI + GROUPS * GROUPS]
        ident = cst[:, C_IDENT:C_IDENT + P]
        ex = sb("ex", [P, 4, 2 * E])
        re = sb("re", [P, 4, 2 * E])
        fea = sb("fea", [P, 4, 2 * E])
        vaug = sb("vaug", [P, 4, HEADS, HA])
        pr = sb("pr", [P, 2, HEADS, HA, HD])
        qs = sb("qs", [P, 2, HEADS, HA, HD])
        hs = sb("hs", [P, 2, HEADS * HA, HD // 2])
        qt = sb("qt", [P, 2, P])
        num = sb("num", [P, 2, HEADS, HA])
        nsum = sb("nsum", [P, 2, HEADS, HA])
        sm = sb("sm", [P, 4, HEADS * HA])
        den = sb("den", [P, 2, HEADS])
        rden = sb("rden", [P, 2, HEADS])
        ao = sb("ao", [P, 2, E])
        aot = sb("aot", [P, 2, E])
        xa = sb("xa", [P, TPB, E])
        bns = sb("bns", [P, TPB, 6])
        st = sb("st", [P, TPB, 5])
        mean = sb("mean", [P, TPB])
        vare = sb("vare", [P, TPB])
        std = sb("std", [P, TPB])
        rstd = sb("rstd", [P, TPB])
        x1s = sb("x1s", [P, TPB, E])
        x1ts = sb("x1ts", [P, TPB * P])
        x1 = sb("x1", [P, NT, E])
        x1th = sb("x1th", [P, TOK], f32r)
        x1tl = sb("x1tl", [P, TOK], f32r)
        lg = sb("lg", [P, NT, NE])
        sc = sb("sc", [P, NT, NE])
        sfc = sb("sfc", [P, NT * GROUPS, GE])
        ta = sb("ta", [P, NT * GROUPS, 4])
        tb = sb("tb", [P, NT * GROUPS, 4])
        tc = sb("tc", [P, NT * GROUPS, 2])
        td = sb("td", [P, NT * GROUPS, 2])
        te = sb("te", [P, NT * GROUPS, 2])
        tf = sb("tf", [P, NT * GROUPS, 1])
        gs = sb("gs", [P, NT, GROUPS])
        c1 = sb("c1", [P, NT, GROUPS * GROUPS])
        c2 = sb("c2", [P, NT, GROUPS * GROUPS])
        rank = sb("rank", [P, NT * GROUPS])
        top = sb("top", [P, NT, TOPK])
        wsum = sb("wsum", [P, NT])
        rw2 = sb("rw2", [P, NT, 2, NE])
        rt = sb("rt", [P, TOK], f32r)
        raw = sb("raw", [P, 2, CW])
        wh = sb("wh", [P, 2, CW], f32r)
        wl = sb("wl", [P, 2, 3 * P], f32r)
        sg = sb("sg", [P, 4, 512])
        ug = sb("ug", [P, 4, 512])
        hh = sb("hh", [P, 4, 512])
        hhi = sb("hhi", [P, 4, 512], f32r)
        hlo = sb("hlo", [P, 4, 512], f32r)
        osb = sb("osb", [P, QB, 512])
        z = sb("z", [P, NT, E])
        bns2 = sb("bns2", [P, NT, 6])
        mv2 = sb("mv2", [P, NT, 2])
        vare2 = sb("vare2", [P, NT])
        std2 = sb("std2", [P, NT])
        rstd2 = sb("rstd2", [P, NT])
        yo = xtok

        bank = [ctx.enter_context(nc.psum_tensor(f"bank{i}", [P, 512], f32)) for i in range(8)]
        pj, sbk, ob, tbk = bank[0], bank[1], bank[2], bank[3]
        cum = bank[4:7]
        ou = bank[0:4]
        gbk = [bank[4], bank[7]]
        ubk, rbk = bank[5], bank[6]

        s_cst = sem("s_cst")
        s_xtok = sem("s_xtok")
        s_xt = [sem(f"s_xt{i}") for i in range(4)]
        s_ones = sem("s_ones")
        s_proj = sem("s_proj")
        s_ex = sem("s_ex")
        s_re = sem("s_re")
        s_fea = sem("s_fea")
        s_vev = sem("s_vev")
        s_pr = sem("s_pr")
        s_cum = sem("s_cum")
        s_qs = sem("s_qs")
        s_hs = sem("s_hs")
        s_num = sem("s_num")
        s_nsum = sem("s_nsum")
        s_qt = sem("s_qt")
        s_qte = sem("s_qte")
        s_o = sem("s_o")
        s_st = sem("s_st")
        s_sm = sem("s_sm")
        s_den = sem("s_den")
        s_rden = sem("s_rden")
        s_ao = sem("s_ao")
        s_aot = sem("s_aot")
        s_aote = sem("s_aote")
        s_y = sem("s_y")
        s_xa = sem("s_xa")
        s_bn = sem("s_bn")
        s_mv = sem("s_mv")
        s_vare = sem("s_vare")
        s_std = sem("s_std")
        s_rstd = sem("s_rstd")
        s_x1 = sem("s_x1")
        s_x1c = sem("s_x1c")
        s_x1t = sem("s_x1t")
        s_x1te = sem("s_x1te")
        s_x1h = sem("s_x1h")
        s_x1l = sem("s_x1l")
        s_lg = sem("s_lg")
        s_lge = sem("s_lge")
        s_sig = sem("s_sig")
        s_rch = sem("s_rch")
        s_rw = sem("s_rw")
        s_rtt = sem("s_rtt")
        s_rte = sem("s_rte")
        s_raw = [sem(f"s_raw{i}") for i in range(2)]
        s_wh = sem("s_wh")
        s_wl = sem("s_wl")
        s_g = sem("s_g")
        s_u = sem("s_u")
        s_r = sem("s_r")
        s_silu = sem("s_silu")
        s_ug = sem("s_ug")
        s_h = sem("s_h")
        s_hhi = sem("s_hhi")
        s_hlo = sem("s_hlo")
        s_d = sem("s_d")
        s_osb = sem("s_osb")
        s_ot = sem("s_ot")
        s_z = sem("s_z")
        s_bn2 = sem("s_bn2")
        s_mv2 = sem("s_mv2")
        s_va2 = sem("s_va2")
        s_sd2 = sem("s_sd2")
        s_rs2 = sem("s_rs2")
        s_yo = sem("s_yo")
        s_out = sem("s_out")

        block = ctx.enter_context(nc.Block())

        @block.sync
        def _(sp):
            def load_x(t, b, c):
                sp.dma_start(xt[:, c, :], x_t[:, ds(t * P, P)]).then_inc(s_xt[c], 16)

            for c in range(4):
                load_x(c, 0, c)
                if c == 0:
                    sp.dma_start(wqkv[:, :], w_qkv).then_inc(s_cst, 16)
                    sp.dma_start(cst[:, :], consts).then_inc(s_cst, 16)
            sp.dma_start(wo[:, :], w_out).then_inc(s_cst, 16)
            sp.dma_start(gw[:, :], gate_w).then_inc(s_cst, 16)
            sp.dma_start(bias[:, :], gate_bias).then_inc(s_cst, 16)
            sp.dma_start(xtok[:, :, :], x_tok).then_inc(s_xtok, 16)
            for ci in range(2):
                sp.dma_start(raw[:, ci, :], w_chunks[ci]).then_inc(s_raw[ci], 16)
            with sp.Fori(1, BATCH) as b:
                for c in range(4):
                    sp.wait_ge(s_proj, 4 * b + c - 3)
                    load_x(4 * b + c, b, c)
            with sp.Fori(1, NCH // 2) as i:
                for k in range(2):
                    sp.wait_ge(s_wh, 2 * i + k - 1)
                    sp.wait_ge(s_wl, 2 * i + k - 1)
                    sp.dma_start(raw[:, k, :], w_chunks[ds(2 * i + k, 1)].rearrange("a p n -> p (a n)"))\
                      .then_inc(s_raw[k], 16)
            for n in range(QB):
                sp.wait_ge(s_yo, 4 * (n + 1))
                sp.dma_start(out[:, 4 * n:4 * n + 4, :], yo[:, 4 * n:4 * n + 4, :]).then_inc(s_out, 16)
            sp.wait_ge(s_out, 16 * QB)

        @block.gpsimd
        def _(pool):
            for c in range(4):
                pool.memset(vaug[:, c, :, HD:HA], 1.0).then_inc(s_ones, 1)
            pool.sem_inc(s_x1l, 1)

            def outer(t, c, k):
                pool.wait_ge(s_fea, t + 1)
                pool.wait_ge(s_vev, t + 1)
                nc.gpsimd.tensor_tensor(
                    pr[:, k], fea[:, c, E:2 * E].rearrange("p (h d) -> p h d", h=HEADS).unsqueeze(2)
                    .to_broadcast([P, HEADS, HA, HD]),
                    vaug[:, c].unsqueeze(3).to_broadcast([P, HEADS, HA, HD]), ALU.mult).then_inc(s_pr, 1)

            def pairs(t, k):
                pool.wait_ge(s_qs, 3 * t + 3)
                v = qs[:, k].rearrange("p h a d -> p (h a) d")
                nc.gpsimd.tensor_tensor(hs[:, k], v[:, :, 0:HD // 2], v[:, :, HD // 2:HD], ALU.add)\
                    .then_inc(s_hs, 1)

            def finish(b):
                pool.wait_ge(s_x1, 4 * b + 4)
                nc.gpsimd.tensor_copy(x1[:, ds(4 * b, 4), :], x1s[:, :, :]).then_inc(s_x1c, 1)
                pool.wait_ge(s_x1te, b + 1)
                pool.wait_ge(s_x1h, b + 1)
                nc.gpsimd.tensor_tensor(x1tl[:, ds(512 * b, 512)], x1ts[:, :],
                                        x1th[:, ds(512 * b, 512)].bitcast(f32), ALU.subtract)\
                    .then_inc(s_x1l, 1)

            def batch(b, first, last):
                for c in range(4):
                    t = 4 * b + c
                    if not (last and c >= 2):
                        outer(t + 2, (c + 2) % 4, c % 2)
                    if not (last and c == 3):
                        pairs(t + 1, (c + 1) % 2)
                    if c == 1 and not first:
                        finish(b - 1)

            outer(0, 0, 0)
            outer(1, 1, 1)
            pairs(0, 0)
            batch(0, True, False)
            with pool.Fori(1, BATCH - 1) as b:
                batch(b, False, False)
            batch(BATCH - 1, False, True)
            finish(BATCH - 1)

            def split_weights(ci, k, i):
                pool.wait_ge(s_wh, ci + 1)
                nc.gpsimd.tensor_tensor(wl[:, k, :], raw[:, k, 0:3 * P], wh[:, k, 0:3 * P].bitcast(f32),
                                        ALU.subtract).then_inc(s_wl, 1)

            def chunk(ci, k, last):
                for n in range(QB):
                    pool.wait_ge(s_hhi, 4 * ci + n + 1)
                    nc.gpsimd.tensor_tensor(hlo[:, n, :], hh[:, n, :], hhi[:, n, :].bitcast(f32),
                                            ALU.subtract).then_inc(s_hlo, 1)
                    if n == 1 and not last:
                        split_weights(ci + 1, 1 - k, 0)

            split_weights(0, 0, 0)
            for ci in range(SC):
                chunk(ci, ci % 2, False)
            with pool.Fori(1, NCH // 2 - 1) as i:
                for k in range(2):
                    chunk(2 * i + k, k, False)
            chunk(NCH - 2, 0, False)
            chunk(NCH - 1, 1, True)

        @block.scalar
        def _(act):
            act.wait_ge(s_ones, 4)

            def exps(t, c):
                act.wait_ge(s_proj, t + 1)
                nc.scalar.activation(ex[:, c, :], pj[:, 0:2 * E], ACT.Exp).then_inc(s_ex, 1)
                nc.scalar.activation(re[:, c, :], pj[:, 0:2 * E], ACT.Relu).then_inc(s_re, 1)
                nc.scalar.activation(vaug[:, c, :, 0:HD],
                                     pj[:, 2 * E:3 * E].rearrange("p (h d) -> p h d", h=HEADS), ACT.Copy)\
                    .then_inc(s_vev, 1)

            def query(t, k):
                act.wait_ge(s_qt, t + 1)
                nc.scalar.activation(qt[:, k, :], tbk[:, 2 * P:3 * P], ACT.Copy).then_inc(s_qte, 1)

            def out_transpose(t, k):
                act.wait_ge(s_aot, t + 1)
                nc.scalar.activation(aot[:, k, :], tbk[:, 0:P], ACT.Copy).then_inc(s_aote, 1)

            def deviation(b):
                act.wait_ge(s_vare, b + 1)
                nc.scalar.activation(std[:, :], vare[:, :], ACT.Sqrt).then_inc(s_std, 1)

            def finish(b):
                act.wait_ge(s_x1t, b + 1)
                act.wait_ge(s_x1l, b + 1)
                nc.scalar.activation(x1ts[:, :], tbk[:, :], ACT.Copy).then_inc(s_x1te, 1)
                nc.scalar.activation(x1th[:, ds(512 * b, 512)], tbk[:, :], ACT.Copy).then_inc(s_x1h, 1)
                act.wait_ge(s_lg, b + 1)
                nc.scalar.activation(lg[:, ds(4 * b, 4), :],
                                     tbk[:, 0:4 * NE].rearrange("p (c e) -> p c e", c=4), ACT.Copy)\
                    .then_inc(s_lge, 1)

            def batch(b, first, last):
                for c in range(4):
                    t = 4 * b + c
                    if not (last and c >= 2):
                        exps(t + 2, (c + 2) % 4)
                    if not (last and c == 3):
                        query(t + 1, (c + 1) % 2)
                    if not (first and c == 0):
                        out_transpose(t - 1, (c + 1) % 2)
                    if c == 0 and not first:
                        deviation(b - 1)
                    if c == 1 and not first:
                        finish(b - 1)

            exps(0, 0)
            exps(1, 1)
            query(0, 0)
            batch(0, True, False)
            with act.Fori(1, BATCH - 1) as b:
                batch(b, False, False)
            batch(BATCH - 1, False, True)
            out_transpose(NT - 1, 1)
            deviation(BATCH - 1)
            finish(BATCH - 1)
            act.wait_ge(s_lge, BATCH)
            nc.scalar.activation(sc[:, :, :], lg[:, :, :], ACT.Sigmoid).then_inc(s_sig, 1)

            def split_weights(ci, k, loaded):
                act.wait_ge(s_raw[k], loaded)
                nc.scalar.activation(wh[:, k, :], raw[:, k, :], ACT.Copy).then_inc(s_wh, 1)

            def upper(u, n):
                act.wait_ge(s_h, u + 1)
                nc.scalar.activation(hhi[:, n, :], hh[:, n, :], ACT.Copy).then_inc(s_hhi, 1)

            def chunk(ci, k, i, first, last):
                for n in range(QB):
                    u = 4 * ci + n
                    if n == 2 and not last:
                        if not first:
                            act.wait_ge(s_d, 4 * ci)
                        split_weights(ci + 1, 1 - k, 16 * (i + 1) if k == 0 else 16 * (i + 2))
                    act.wait_ge(s_g, u + 1)
                    nc.scalar.activation(sg[:, n, :], gbk[n % 2][:, :], ACT.Silu).then_inc(s_silu, 1)
                    if not (first and n == 0):
                        upper(u - 1, (n + 3) % 4)

            split_weights(0, 0, 16)
            chunk(0, 0, 0, True, False)
            chunk(1, 1, 0, False, False)
            for n in range(QB):
                act.wait_ge(s_rtt, n + 1)
                nc.scalar.activation(rt[:, 512 * n:512 * n + 512], rbk[:, :], ACT.Copy).then_inc(s_rte, 1)
            with act.Fori(1, NCH // 2 - 1) as i:
                for k in range(2):
                    chunk(2 * i + k, k, i, False, False)
            chunk(NCH - 2, 0, NCH // 2 - 1, False, False)
            chunk(NCH - 1, 1, NCH // 2 - 1, False, True)
            upper(4 * NCH - 1, 3)
            for n in range(QB):
                act.wait_ge(s_d, 4 * NCH - 3 + n)
                nc.scalar.activation(osb[:, n, :], ou[n][:, :], ACT.Copy).then_inc(s_osb, 1)
            for n in range(QB):
                act.wait_ge(s_va2, n + 1)
                nc.scalar.activation(std2[:, 4 * n:4 * n + 4], vare2[:, 4 * n:4 * n + 4], ACT.Sqrt)\
                    .then_inc(s_sd2, 1)

        @block.vector
        def _(dve):
            V = nc.vector
            dve.wait_ge(s_cst, 80)

            def elu(t, c):
                dve.wait_ge(s_re, t + 1)
                V.scalar_tensor_tensor(fea[:, c, :], ex[:, c, :], 1.0, re[:, c, :], ALU.min, ALU.add)\
                    .then_inc(s_fea, 1)

            def times_q(t, c, k):
                for j, (h0, m) in enumerate(THIRDS):
                    dve.wait_ge(s_cum, 3 * t + j + 1)
                    V.tensor_tensor(qs[:, k, h0:h0 + m],
                                    cum[j][:, 0:HP * m].rearrange("p (h a d) -> p h a d", h=m, a=HA),
                                    fea[:, c, HD * h0:HD * (h0 + m)].rearrange("p (h d) -> p h d", h=m)
                                    .unsqueeze(2).to_broadcast([P, m, HA, HD]), ALU.mult).then_inc(s_qs, 1)

            def state(b, c):
                dve.wait_ge(s_st, 3 * b + c + 1)
                V.tensor_tensor(sm[:, c, :], sbk[:, 0:HEADS * HA], bmask, ALU.mult).then_inc(s_sm, 1)

            def divide(t, b, c, k):
                dve.wait_ge(s_hs, t + 1)
                V.tensor_reduce(num[:, k].rearrange("p h a -> p (h a)"), hs[:, k], AX.X, ALU.add)\
                    .then_inc(s_num, 1)
                dve.wait_ge(s_num, t + 1)
                o = num[:, k]
                if c:
                    dve.wait_ge(s_o, 3 * b + c)
                    V.tensor_tensor(nsum[:, k], ob[:, 0:HEADS * HA].rearrange("p (h a) -> p h a", h=HEADS),
                                    num[:, k], ALU.add).then_inc(s_nsum, 1)
                    dve.wait_ge(s_nsum, 3 * b + c)
                    o = nsum[:, k]
                V.tensor_scalar(den[:, k, :].unsqueeze(2), o[:, :, HD:HA], 1e-6, None, ALU.max).then_inc(s_den, 1)
                dve.wait_ge(s_den, t + 1)
                V.reciprocal(rden[:, k, :], den[:, k, :]).then_inc(s_rden, 1)
                dve.wait_ge(s_rden, t + 1)
                V.tensor_tensor(ao[:, k, :].rearrange("p (h d) -> p h d", h=HEADS), o[:, :, 0:HD],
                                rden[:, k, :].unsqueeze(2).to_broadcast([P, HEADS, HD]), ALU.mult)\
                    .then_inc(s_ao, 1)

            def residual(t, c):
                dve.wait_ge(s_y, t + 1)
                V.tensor_tensor(xa[:, c, :], tbk[:, P:2 * P], xtok[:, ds(t, 1), :].rearrange("p a e -> p (a e)"),
                                ALU.add).then_inc(s_xa, 1)
                dve.wait_ge(s_xa, t + 1)
                V.bn_stats(bns[:, c, :], xa[:, c, :]).then_inc(s_bn, 1)

            def finish_a(b):
                half = E // 2
                dve.wait_ge(s_bn, 4 * b + 4)
                V.tensor_tensor(st[:, :, 0:1], bns[:, :, 1:2], bns[:, :, 4:5], ALU.add).then_inc(s_mv, 1)
                V.tensor_tensor(st[:, :, 1:2], bns[:, :, 1:2], bns[:, :, 4:5], ALU.subtract).then_inc(s_mv, 1)
                V.tensor_tensor(st[:, :, 2:3], bns[:, :, 2:3], bns[:, :, 5:6], ALU.add).then_inc(s_mv, 1)
                dve.wait_ge(s_mv, 6 * b + 3)
                V.tensor_scalar(mean[:, :].unsqueeze(2), st[:, :, 0:1], 0.5, None, ALU.mult).then_inc(s_mv, 1)
                V.tensor_tensor(st[:, :, 3:4], st[:, :, 1:2], st[:, :, 1:2], ALU.mult).then_inc(s_mv, 1)
                V.tensor_scalar(st[:, :, 4:5], st[:, :, 2:3], 0.5 / half, 1e-5, ALU.mult, ALU.add).then_inc(s_mv, 1)
                dve.wait_ge(s_mv, 6 * b + 6)
                V.scalar_tensor_tensor(vare[:, :].unsqueeze(2), st[:, :, 3:4], 0.25, st[:, :, 4:5],
                                       ALU.mult, ALU.add).then_inc(s_vare, 1)

            def finish_b(b):
                dve.wait_ge(s_std, b + 1)
                V.reciprocal(rstd[:, :], std[:, :]).then_inc(s_rstd, 1)
                dve.wait_ge(s_rstd, b + 1)
                dve.wait_ge(s_x1l, b + 1)
                for c in range(4):
                    V.tensor_scalar(x1s[:, c, :], xa[:, c, :], mean[:, c:c + 1], rstd[:, c:c + 1],
                                    ALU.subtract, ALU.mult).then_inc(s_x1, 1)

            def batch(b, first, last):
                for c in range(4):
                    t = 4 * b + c
                    divide(t, b, c, c % 2)
                    if not (last and c >= 2):
                        elu(t + 2, (c + 2) % 4)
                    if not (last and c == 3):
                        times_q(t + 1, (c + 1) % 4, (c + 1) % 2)
                    if c < 3:
                        state(b, c)
                    if c == 0 and not first:
                        residual(t - 1, 3)
                        finish_a(b - 1)
                        finish_b(b - 1)
                    elif c:
                        residual(t - 1, c - 1)

            elu(0, 0)
            elu(1, 1)
            times_q(0, 0, 0)
            dve.wait_ge(s_xtok, 16)
            batch(0, True, False)
            with dve.Fori(1, BATCH - 1) as b:
                batch(b, False, False)
            batch(BATCH - 1, False, True)
            residual(NT - 1, 3)
            finish_a(BATCH - 1)
            finish_b(BATCH - 1)

            steps = [0]

            def step(ins):
                steps[0] += 1
                ins.then_inc(s_rch, 1)

            def after():
                dve.wait_ge(s_rch, steps[0])

            def shared_unit(u):
                n = u % 4
                dve.wait_ge(s_silu, u + 1)
                dve.wait_ge(s_u, u + 1)
                V.tensor_tensor(hh[:, n, :], ubk[:, :], sg[:, n, :], ALU.mult).then_inc(s_h, 1)

            dve.wait_ge(s_sig, 1)
            sview = sfc[:, :, :].rearrange("p (t g) e -> p t (g e)", t=NT)
            step(V.tensor_tensor(sview, sc[:, :, :], bias[:, :].unsqueeze(1).to_broadcast([P, NT, NE]), ALU.add))
            shared_unit(0)
            after()
            step(V.tensor_tensor(ta[:, :, :], sfc[:, :, 0:4], sfc[:, :, 4:8], ALU.max))
            step(V.tensor_tensor(tb[:, :, :], sfc[:, :, 0:4], sfc[:, :, 4:8], ALU.min))
            shared_unit(1)
            after()
            step(V.tensor_tensor(tc[:, :, :], ta[:, :, 0:2], ta[:, :, 2:4], ALU.max))
            step(V.tensor_tensor(td[:, :, :], ta[:, :, 0:2], ta[:, :, 2:4], ALU.min))
            step(V.tensor_tensor(te[:, :, :], tb[:, :, 0:2], tb[:, :, 2:4], ALU.max))
            after()
            step(V.tensor_tensor(te[:, :, :], te[:, :, :], td[:, :, :], ALU.max))
            after()
            step(V.tensor_tensor(ta[:, :, 0:1], tc[:, :, 0:1], tc[:, :, 1:2], ALU.max))
            step(V.tensor_tensor(tb[:, :, 0:1], tc[:, :, 0:1], tc[:, :, 1:2], ALU.min))
            step(V.tensor_tensor(tf[:, :, :], te[:, :, 0:1], te[:, :, 1:2], ALU.max))
            after()
            step(V.tensor_tensor(tb[:, :, 0:1], tb[:, :, 0:1], tf[:, :, :], ALU.max))
            after()
            gsv = gs[:, :, :].rearrange("p t g -> p (t g)")
            step(V.tensor_tensor(gsv.unsqueeze(2), ta[:, :, 0:1], tb[:, :, 0:1], ALU.add))
            shared_unit(2)
            c1v = c1[:, :, :].rearrange("p t (i j) -> p t i j", i=GROUPS)
            c2v = c2[:, :, :].rearrange("p t (i j) -> p t i j", i=GROUPS)
            gj = gs[:, :, :].unsqueeze(2).to_broadcast([P, NT, GROUPS, GROUPS])
            gi = gs[:, :, :].unsqueeze(3).to_broadcast([P, NT, GROUPS, GROUPS])
            after()
            step(V.tensor_tensor(c1v, gj, gi, ALU.is_equal))
            step(V.tensor_tensor(c2v, gj, gi, ALU.is_gt))
            shared_unit(3)
            after()
            step(V.tensor_tensor(c1[:, :, :], c1[:, :, :],
                                 tri.unsqueeze(1).to_broadcast([P, NT, GROUPS * GROUPS]), ALU.mult))
            after()
            step(V.tensor_tensor(c1[:, :, :], c1[:, :, :], c2[:, :, :], ALU.add))
            shared_unit(4)
            after()
            step(V.tensor_reduce(rank[:, :], c1[:, :, :].rearrange("p t (i j) -> p (t i) j", i=GROUPS),
                                 AX.X, ALU.add))
            after()
            step(V.tensor_scalar(rank[:, :], rank[:, :], float(TOPG), None, ALU.is_lt))
            after()
            step(V.tensor_tensor(sfc[:, :, :], sfc[:, :, :],
                                 rank[:, :].unsqueeze(2).to_broadcast([P, NT * GROUPS, GE]), ALU.mult))
            shared_unit(5)
            after()
            step(V.tensor_scalar(sfc[:, :, :], sfc[:, :, :], 0.0, None, ALU.add))
            after()
            for t in range(NT):
                step(V.max(top[:, t, :], sview[:, t, :]))
            shared_unit(6)
            after()
            for t in range(NT):
                step(V.match_replace(lg[:, t, :], top[:, t, :], sview[:, t, :], -3.0e38))
            shared_unit(7)
            after()
            step(V.tensor_tensor(lg[:, :, :], lg[:, :, :], sview, ALU.not_equal))
            after()
            step(V.tensor_tensor(sc[:, :, :], sc[:, :, :], lg[:, :, :], ALU.mult))
            after()
            step(V.tensor_reduce(wsum[:, :], sc[:, :, :], AX.X, ALU.add))
            after()
            step(V.tensor_scalar(wsum[:, :], wsum[:, :], 1e-20, None, ALU.add))
            after()
            step(V.reciprocal(wsum[:, :], wsum[:, :]))
            after()
            step(V.tensor_tensor(sc[:, :, :], sc[:, :, :], wsum[:, :].unsqueeze(2).to_broadcast([P, NT, NE]),
                                 ALU.mult))
            after()
            step(V.tensor_scalar(sc[:, :, :], sc[:, :, :], RSCALE, None, ALU.mult))
            after()
            step(V.tensor_scalar(rw2[:, :, 0, :].bitcast(f32r), sc[:, :, :], 1.0, None, ALU.mult))
            after()
            V.tensor_tensor(rw2[:, :, 1, :], sc[:, :, :], rw2[:, :, 0, :], ALU.subtract).then_inc(s_rw, 1)

            def chunk(ci):
                for n in range(QB):
                    u = 4 * ci + n
                    r = u - 4 * SC
                    dve.wait_ge(s_silu, u + 1)
                    dve.wait_ge(s_u, u + 1)
                    V.tensor_tensor(ug[:, n, :], ubk[:, :], sg[:, n, :], ALU.mult).then_inc(s_ug, 1)
                    dve.wait_ge(s_ug, r + 1)
                    dve.wait_ge(s_r, r + 1)
                    V.tensor_tensor(hh[:, n, :], rbk[:, :], ug[:, n, :], ALU.mult).then_inc(s_h, 1)

            with dve.Fori(1, NCH // 2) as i:
                for k in range(2):
                    chunk(2 * i + k)

            for n in range(QB):
                dve.wait_ge(s_ot, n + 1)
                q = slice(4 * n, 4 * n + 4)
                V.tensor_tensor(z[:, q, :], bank[4 + n][:, :].rearrange("p (c e) -> p c e", c=4), x1[:, q, :],
                                ALU.add).then_inc(s_z, 1)
                dve.wait_ge(s_z, n + 1)
                for t in range(4 * n, 4 * n + 4):
                    V.bn_stats(bns2[:, t, :], z[:, t, :]).then_inc(s_bn2, 1)
                for t in range(4 * n, 4 * n + 4):
                    dve.wait_ge(s_bn2, t + 1)
                    V.bn_aggr(mv2[:, t, :], bns2[:, t, :]).then_inc(s_mv2, 1)
                dve.wait_ge(s_mv2, 4 * n + 4)
                V.tensor_scalar(vare2[:, q].unsqueeze(2), mv2[:, q, 1:2], 1e-5, None, ALU.add).then_inc(s_va2, 1)
            for n in range(QB):
                q = slice(4 * n, 4 * n + 4)
                dve.wait_ge(s_sd2, n + 1)
                V.reciprocal(rstd2[:, q], std2[:, q]).then_inc(s_rs2, 1)
                dve.wait_ge(s_rs2, n + 1)
                for t in range(4 * n, 4 * n + 4):
                    V.tensor_scalar(yo[:, t, :], z[:, t, :], mv2[:, t, 0:1], rstd2[:, t:t + 1],
                                    ALU.subtract, ALU.mult).then_inc(s_yo, 1)

        @block.tensor
        def _(pe):
            mm = nc.tensor.matmul

            def project(t, c, nth, first):
                pe.wait_ge(s_xt[c], 16 * nth)
                if not first:
                    pe.wait_ge(s_vev, t)
                mm(pj[:, 0:3 * E], xt[:, c, :], wqkv[:, :], start=True, stop=True).then_inc(s_proj, 1)

            def running(t, k, first):
                pe.wait_ge(s_pr, t + 1)
                for j, (h0, m) in enumerate(THIRDS):
                    if not first:
                        pe.wait_ge(s_qs, 3 * t + j - 2)
                    mm(cum[j][:, 0:HP * m], causal, pr[:, k, h0:h0 + m].rearrange("p h a d -> p (h a d)"),
                       start=True, stop=True).then_inc(s_cum, 1)

            def query(t, c, read):
                pe.wait_ge(s_fea, t + 1)
                if read is not None:
                    pe.wait_ge(s_xa, read)
                nc.tensor.transpose(tbk[:, 2 * P:3 * P], fea[:, c, 0:E], ident).then_inc(s_qt, 1)

            def sums(b, c, first):
                t = 4 * b + c
                if c:
                    pe.wait_ge(s_qte, t + 1)
                    pe.wait_ge(s_sm, 3 * b + c)
                    if not (first and c == 1):
                        pe.wait_ge(s_nsum, 3 * b + c - 1)
                    mm(ob[:, 0:HEADS * HA], qt[:, c % 2, :], sm[:, c - 1, :], start=True, stop=True)\
                        .then_inc(s_o, 1)
                if c < 3:
                    if c == 0 and not first:
                        pe.wait_ge(s_sm, 3 * b)
                    elif c == 0:
                        pe.wait_ge(s_vev, t + 1)
                        pe.wait_ge(s_fea, t + 1)
                    mm(sbk[:, 0:HEADS * HA], fea[:, c, E:2 * E],
                       vaug[:, c].rearrange("p h a -> p (h a)"), start=(c == 0), stop=True,
                       skip_group_check=True).then_inc(s_st, 1)

            def output(t, k, later, first=False):
                pe.wait_ge(s_ao, t + 1)
                if not first:
                    pe.wait_ge(s_xa, t)
                pe.wait_ge(s_qte, later)
                nc.tensor.transpose(tbk[:, 0:P], ao[:, k, :], ident).then_inc(s_aot, 1)
                pe.wait_ge(s_aote, t + 1)
                mm(tbk[:, P:2 * P], aot[:, k, :], wo[:, :], start=True, stop=True).then_inc(s_y, 1)

            def finish(b):
                pe.wait_ge(s_x1, 4 * b + 4)
                for c in range(4):
                    last = nc.tensor.transpose(tbk[:, P * c:P * c + P], x1s[:, c, :], ident)
                last.then_inc(s_x1t, 1)
                pe.wait_ge(s_x1te, b + 1)
                pe.wait_ge(s_x1h, b + 1)
                for c in range(4):
                    last = mm(tbk[:, NE * c:NE * c + NE], x1ts[:, P * c:P * c + P], gw[:, :], start=True, stop=True)
                last.then_inc(s_lg, 1)

            def batch(b, first, last):
                for c in range(4):
                    t = 4 * b + c
                    if not (last and c >= 2):
                        project(t + 2, (c + 2) % 4, b + 1 + (c >= 2), False)
                    sums(b, c, first)
                    if c == 2 and not first:
                        pe.wait_ge(s_lge, b)
                    if not (last and c == 3):
                        pe.wait_ge(s_qte, t + 1)
                        query(t + 1, (c + 1) % 4, None if first and c < 2 else t - 1)
                        running(t + 1, (c + 1) % 2, False)
                    if not (first and c == 0):
                        output(t - 1, (c + 1) % 2, NT if last and c == 3 else t + 2, first and c == 1)
                    if c == 1 and not first:
                        pe.wait_ge(s_xa, t)
                        finish(b - 1)

            pe.wait_ge(s_cst, 80)
            project(0, 0, 1, True)
            project(1, 1, 1, False)
            query(0, 0, None)
            running(0, 0, True)
            batch(0, True, False)
            with pe.Fori(1, BATCH - 1) as b:
                batch(b, False, False)
            batch(BATCH - 1, False, True)
            output(NT - 1, 1, NT)
            finish(BATCH - 1)

            def product(dst, k, col, hi, lo, start, stop):
                mm(dst, wh[:, k, col:col + P], hi, start=start, stop=False, skip_group_check=True)
                mm(dst, wh[:, k, col:col + P], lo, start=False, stop=False, skip_group_check=True)
                return mm(dst, wl[:, k, col:col + P], hi, start=False, stop=stop, skip_group_check=True)

            def down(u, k, n, start):
                pe.wait_ge(s_hlo, u + 1)
                product(ou[n][:, :], k, 2 * P, hhi[:, n, :], hlo[:, n, :], start, True).then_inc(s_d, 1)

            def chunk(ci, k, routed, first_ever=False, first_routed=False, start_banks=False):
                pe.wait_ge(s_wh, ci + 1)
                pe.wait_ge(s_wl, ci + 1)
                for n in range(QB):
                    u = 4 * ci + n
                    r = u - 4 * SC
                    xs = slice(512 * n, 512 * n + 512)
                    if not (first_ever and n < 2):
                        pe.wait_ge(s_silu, u - 1)
                    product(gbk[n % 2][:, :], k, 0, x1th[:, xs], x1tl[:, xs], True, True).then_inc(s_g, 1)
                    if not routed or (first_routed and n == 0):
                        if not (first_ever and n == 0):
                            pe.wait_ge(s_h, u)
                    else:
                        pe.wait_ge(s_ug, r)
                    product(ubk[:, :], k, P, x1th[:, xs], x1tl[:, xs], True, True).then_inc(s_u, 1)
                    if routed:
                        pe.wait_ge(s_h, u)
                        mm(rbk[:, :], wh[:, k, 3 * P:4 * P], rt[:, xs], start=True, stop=True).then_inc(s_r, 1)
                    if not (first_ever and n < 2):
                        down(u - 2, k if n >= 2 else 1 - k, (n + 2) % 4,
                             first_ever or (start_banks and n < 2))

            pe.wait_ge(s_lge, BATCH)
            pe.wait_ge(s_x1l, BATCH + 1)
            chunk(0, 0, False, first_ever=True)
            chunk(1, 1, False, start_banks=True)
            pe.wait_ge(s_rw, 1)
            for n in range(QB):
                if n:
                    pe.wait_ge(s_rte, n)
                for c in range(4):
                    last = nc.tensor.transpose(rbk[:, P * c:P * c + P],
                                               rw2[:, 4 * n + c].rearrange("p a e -> p (a e)"), ident)
                last.then_inc(s_rtt, 1)
            pe.wait_ge(s_rte, QB)
            chunk(2, 0, True, first_routed=True)
            chunk(3, 1, True)
            with pe.Fori(2, NCH // 2) as i:
                for k in range(2):
                    chunk(2 * i + k, k, True)
            down(4 * NCH - 2, 1, 2, False)
            down(4 * NCH - 1, 1, 3, False)
            for n in range(QB):
                pe.wait_ge(s_osb, n + 1)
                if n == 0:
                    pe.wait_ge(s_h, 4 * NCH)
                for c in range(4):
                    last = nc.tensor.transpose(bank[4 + n][:, P * c:P * c + P], osb[:, n, P * c:P * c + P], ident)
                last.then_inc(s_ot, 1)


def layouts(L0_attn_x, L0_attn_W_qkv, L0_attn_W_out, L0_ffn_gate_w, L0_ffn_gate_bias, L0_ffn_Wg, L0_ffn_Wu,
            L0_ffn_Wd, L0_ffn_Sg, L0_ffn_Su, L0_ffn_Sd):
    import numpy as np

    x = np.asarray(L0_attn_x).reshape(TOK, E)
    chunks = np.zeros((NCH, P, CW), np.float32)

    def rows_to_columns(w, first, count, at):
        full = np.zeros((count * P, E), np.float32)
        full[:w.shape[0]] = w
        chunks[first:first + count, :, at:at + P] = full.reshape(count, P, E).transpose(0, 2, 1)

    rows_to_columns(np.asarray(L0_ffn_Sg), 0, SC, 0)
    rows_to_columns(np.asarray(L0_ffn_Su), 0, SC, P)
    rows_to_columns(np.asarray(L0_ffn_Wg).reshape(NE * INTER, E), SC, RC, 0)
    rows_to_columns(np.asarray(L0_ffn_Wu).reshape(NE * INTER, E), SC, RC, P)
    sd = np.zeros((SC * P, E), np.float32)
    sd[:SHARED] = np.asarray(L0_ffn_Sd).T
    chunks[0:SC, :, 2 * P:3 * P] = sd.reshape(SC, P, E)
    chunks[SC:, :, 2 * P:3 * P] = np.asarray(L0_ffn_Wd).transpose(0, 2, 1).reshape(RC, P, E)
    expert = np.arange(NE * INTER) // INTER
    pick = (np.arange(P)[:, None] % NE == expert[None, :]).astype(np.float32)
    chunks[SC:, :, 3 * P:4 * P] = pick.reshape(P, RC, P).transpose(1, 0, 2)

    cst = np.zeros((P, C_END), np.float32)
    p = np.arange(P)
    scale = float(HD) ** -0.5
    cst[:, C_CAUSAL:C_CAUSAL + P] = (p[:, None] <= p[None, :]) * scale
    cst[:, C_BMASK:C_BMASK + HEADS * HA] = (p[:, None] // HD == np.arange(HEADS * HA)[None, :] // HA) * scale
    g = np.arange(GROUPS)
    cst[:, C_TRI:C_TRI + GROUPS * GROUPS] = (g[None, :] < g[:, None]).reshape(1, -1)
    cst[:, C_IDENT:C_IDENT + P] = p[:, None] == p[None, :]
    return {
        "x_tok": np.ascontiguousarray(x.reshape(NT, P, E).transpose(1, 0, 2)),
        "x_t": np.ascontiguousarray(x.T),
        "w_qkv": np.ascontiguousarray(np.asarray(L0_attn_W_qkv).T),
        "w_out": np.ascontiguousarray(np.asarray(L0_attn_W_out).T),
        "gate_w": np.ascontiguousarray(np.asarray(L0_ffn_gate_w).T),
        "gate_bias": np.ascontiguousarray(np.broadcast_to(np.asarray(L0_ffn_gate_bias)[None, :], (P, NE))),
        "w_chunks": chunks,
        "consts": cst,
    }


def kernel(**inputs):
    import concourse.bacc as _bacc
    from concourse.bass_utils import run_bass_kernel_spmd as _run

    nc = _bacc.Bacc("TRN2", target_bir_lowering=False, num_devices=1)
    arrays, args = {}, []
    for name, a in layouts(**inputs).items():
        arrays[f"in_{name}"] = a
        args.append(nc.dram_tensor(f"in_{name}", a.shape, mybir.dt.from_np(a.dtype), kind="ExternalInput").ap())
    o = nc.dram_tensor("out_x", (BATCH, SEQ, E), mybir.dt.float32, kind="ExternalOutput").ap()
    build(nc, *args, o.rearrange("b (j p) e -> p (b j) e", p=P))
    r = _run(nc, [arrays], core_ids=[0])
    return r.results[0]["out_x"]
```

```python
from contextlib import ExitStack

import concourse.bass as bass
from concourse import mybir

TOK, E = 2048, 128
BATCH, SEQ = 4, 512
HEADS, HD = 16, 8
P = 128
NT = TOK // P
TPB = SEQ // P
NE, INTER = 64, 88
SHARED = 2 * INTER
GROUPS, TOPK, TOPG = 8, 8, 4
GE = NE // GROUPS
RSCALE = 2.5
SC = -(-SHARED // P)
RPC = P // NE
RC = INTER // RPC
NCH = SC + RC
SLOTS = 4
AHEAD = 2
ROUNDS = RC // SLOTS
QB = TOK // 512
HA = HD + 1
HP = HA * HD
THIRDS = ((0, 6), (6, 5), (11, 5))
CW = 3 * P
NONE = -3.0e38

C_CAUSAL = 0
C_BMASK = C_CAUSAL + P
C_IDENT = C_BMASK + HEADS * HA
C_END = C_IDENT + P


def build(nc, x_tok, x_t, w_qkv, w_out, gate_w, gate_bias, w_chunks, consts, out):
    f32 = mybir.dt.float32
    f32r = mybir.dt.float32r
    ALU = mybir.AluOpType
    ACT = mybir.ActivationFunctionType
    AX = mybir.AxisListType
    ds = bass.ds

    ctx = ExitStack()
    with ctx:
        def sb(name, shape, dt=f32):
            return ctx.enter_context(nc.sbuf_tensor(name, shape, dt))

        def sem(name):
            return ctx.enter_context(nc.semaphore(name))

        xtok = sb("xtok", [P, NT, E])
        xt = sb("xt", [P, 4, P])
        wqkv = sb("wqkv", [P, 3 * E])
        wo = sb("wo", [P, E])
        gw = sb("gw", [P, NE])
        bias = sb("bias", [P, NE])
        cst = sb("cst", [P, C_END])
        causal = cst[:, C_CAUSAL:C_CAUSAL + P]
        bmask = cst[:, C_BMASK:C_BMASK + HEADS * HA]
        ident = cst[:, C_IDENT:C_IDENT + P]
        warm = sb("warm", [P, 1])
        ex = sb("ex", [P, 4, 2 * E])
        re = sb("re", [P, 4, 2 * E])
        fea = sb("fea", [P, 4, 2 * E])
        vaug = sb("vaug", [P, 4, HEADS, HA])
        pr = sb("pr", [P, 2, HEADS, HA, HD])
        qs = sb("qs", [P, 2, HEADS, HA, HD])
        hs = sb("hs", [P, 2, HEADS * HA, HD // 2])
        qt = sb("qt", [P, 2, P])
        num = sb("num", [P, 2, HEADS, HA])
        nsum = sb("nsum", [P, 2, HEADS, HA])
        sm = sb("sm", [P, 4, HEADS * HA])
        den = sb("den", [P, 2, HEADS])
        rden = sb("rden", [P, 2, HEADS])
        ao = sb("ao", [P, 2, E])
        aot = sb("aot", [P, 2, E])
        xa = sb("xa", [P, TPB, E])
        bns = sb("bns", [P, TPB, 6])
        st = sb("st", [P, TPB, 5])
        mean = sb("mean", [P, TPB])
        vare = sb("vare", [P, TPB])
        std = sb("std", [P, TPB])
        rstd = sb("rstd", [P, TPB])
        shift = sb("shift", [P, TPB])
        x1s = sb("x1s", [P, TPB, E])
        x1ts = sb("x1ts", [P, TPB * P])
        identr = sb("identr", [P, P], f32r)
        x1th = sb("x1th", [P, TOK], f32r)
        x1tl = sb("x1tl", [P, TOK], f32r)
        sc = sb("sc", [P, 2, TPB, NE])
        sfc = sb("sfc", [P, TPB * GROUPS, GE])
        ta = sb("ta", [P, TPB * GROUPS, 4])
        tb = sb("tb", [P, TPB * GROUPS, 4])
        tc = sb("tc", [P, TPB * GROUPS, 2])
        td = sb("td", [P, TPB * GROUPS, 2])
        te = sb("te", [P, TPB * GROUPS, 2])
        tf = sb("tf", [P, TPB * GROUPS, 1])
        gs = sb("gs", [P, TPB, GROUPS])
        gtop = sb("gtop", [P, TPB, GROUPS])
        gtake = sb("gtake", [P, TPB, GROUPS])
        gleft = sb("gleft", [P, TPB, GROUPS])
        gm = sb("gm", [P, TPB * GROUPS])
        sg4 = sb("sg4", [P, TPB * GROUPS, GE])
        top = sb("top", [P, TPB, TOPK])
        left = sb("left", [P, TPB, NE])
        wt = sb("wt", [P, TPB, NE])
        wsum = sb("wsum", [P, 3, TPB])
        rwd = sb("rwd", [P, NT, NE, RPC])
        rt = sb("rt", [P, TOK])
        raw = sb("raw", [P, SLOTS, CW])
        wh = sb("wh", [P, SLOTS, CW], f32r)
        wl = sb("wl", [P, SLOTS, CW], f32r)
        ug = sb("ug", [P, 4, 512])
        hh = sb("hh", [P, 4, 512])
        hhi = sb("hhi", [P, 4, 512], f32r)
        hlo = sb("hlo", [P, 4, 512], f32r)
        osb = sb("osb", [P, QB, 512])
        bns2 = sb("bns2", [P, NT, 6])
        mv2 = sb("mv2", [P, NT, 2])
        vare2 = sb("vare2", [P, NT])
        std2 = sb("std2", [P, NT])
        rstd2 = sb("rstd2", [P, NT])
        shift2 = sb("shift2", [P, NT])
        yo = xtok

        bank = [ctx.enter_context(nc.psum_tensor(f"bank{i}", [P, 512], f32)) for i in range(8)]
        pj, sbk, ob, tbk = bank[0], bank[1], bank[2], bank[3]
        cum = bank[4:7]
        qtb = pj[:, 3 * E:3 * E + P]
        bbk = bank[7]
        tails = [bank[4], bank[5], bank[7], bank[6]]
        ou = bank[0:4]
        gbk = [bank[4], bank[7]]
        ubk = [bank[5], bank[6]]

        s_wqkv = sem("s_wqkv")
        s_cst = sem("s_cst")
        s_small = sem("s_small")
        s_xtok = sem("s_xtok")
        s_x4 = sem("s_x4")
        s_xt = [sem(f"s_xt{i}") for i in range(4)]
        s_ones = sem("s_ones")
        s_warm = sem("s_warm")
        s_proj = sem("s_proj")
        s_ex = sem("s_ex")
        s_re = sem("s_re")
        s_fea = sem("s_fea")
        s_vev = sem("s_vev")
        s_pr = sem("s_pr")
        s_cum = sem("s_cum")
        s_qs = sem("s_qs")
        s_hs = sem("s_hs")
        s_num = sem("s_num")
        s_nsum = sem("s_nsum")
        s_qt = sem("s_qt")
        s_qte = sem("s_qte")
        s_o = sem("s_o")
        s_st = sem("s_st")
        s_sm = sem("s_sm")
        s_den = sem("s_den")
        s_rden = sem("s_rden")
        s_ao = sem("s_ao")
        s_aot = sem("s_aot")
        s_aote = sem("s_aote")
        s_y = sem("s_y")
        s_xa = sem("s_xa")
        s_bn = sem("s_bn")
        s_mv = sem("s_mv")
        s_vare = sem("s_vare")
        s_std = sem("s_std")
        s_rstd = sem("s_rstd")
        s_shift = sem("s_shift")
        s_x1 = sem("s_x1")
        s_x1t = sem("s_x1t")
        s_x1te = sem("s_x1te")
        s_x1h = sem("s_x1h")
        s_x1l = sem("s_x1l")
        s_lg = sem("s_lg")
        s_sig = sem("s_sig")
        s_sfc = sem("s_sfc")
        s_grp = sem("s_grp")
        s_sg4 = sem("s_sg4")
        s_rch = sem("s_rch")
        s_settled = sem("s_settled")
        s_rw = sem("s_rw")
        s_rtt = sem("s_rtt")
        s_idr = sem("s_idr")
        s_rte = sem("s_rte")
        s_raw = [sem(f"s_raw{i}") for i in range(SLOTS)]
        s_wh = sem("s_wh")
        s_wl = sem("s_wl")
        s_g = sem("s_g")
        s_u = sem("s_u")
        s_silu = sem("s_silu")
        s_ur = sem("s_ur")
        s_h = sem("s_h")
        s_hhi = sem("s_hhi")
        s_hlo = sem("s_hlo")
        s_hlo2 = sem("s_hlo2")
        s_d = sem("s_d")
        s_osb = [sem(f"s_osb{n}") for n in range(QB)]
        s_ot = sem("s_ot")
        s_bn2 = sem("s_bn2")
        s_mv2 = sem("s_mv2")
        s_va2 = sem("s_va2")
        s_sd2 = sem("s_sd2")
        s_rs2 = sem("s_rs2")
        s_sh2 = sem("s_sh2")
        s_yo = [sem(f"s_yo{n}") for n in range(QB)]
        s_out = sem("s_out")

        FIRST, SECOND, INNER, LAST = range(4)
        STEPS = 12

        block = ctx.enter_context(nc.Block())

        @block.sync
        def _(sp):
            def load_x(t, b, c):
                sp.dma_start(xt[:, c, :], x_t[:, ds(t * P, P)]).then_inc(s_xt[c], 16)

            sp.dma_start(xt[:, :, :].rearrange("p c t -> p (c t)"), x_t[:, 0:4 * P]).then_inc(s_x4, 16)
            sp.dma_start(cst[:, :], consts).then_inc(s_cst, 16)
            sp.dma_start(wo[:, :], w_out).then_inc(s_small, 16)
            sp.dma_start(gw[:, :], gate_w).then_inc(s_small, 16)
            sp.dma_start(bias[:, :], gate_bias).then_inc(s_small, 16)
            sp.dma_start(xtok[:, :, :], x_tok).then_inc(s_xtok, 16)
            for ci in range(SLOTS):
                sp.dma_start(raw[:, ci, :], w_chunks[ci]).then_inc(s_raw[ci], 16)
            with sp.Fori(1, BATCH) as b:
                for c in range(4):
                    sp.wait_ge(s_proj, 4 * b + c - 3)
                    load_x(4 * b + c, b, c)

            def load_chunk(ci, k):
                sp.wait_ge(s_wh, ci - SLOTS + 1)
                sp.wait_ge(s_wl, ci - SLOTS + 1)
                sp.dma_start(raw[:, k, :], w_chunks[ds(ci, 1)].rearrange("a p n -> p (a n)"))\
                  .then_inc(s_raw[k], 16)

            with sp.Fori(1, NCH // SLOTS) as i:
                for k in range(SLOTS):
                    load_chunk(SLOTS * i + k, k)
            for k in range(NCH % SLOTS):
                load_chunk(NCH - NCH % SLOTS + k, k)
            for n in range(2):
                sp.wait_ge(s_yo[n], 4)
                sp.dma_start(out[:, 4 * n:4 * n + 4, :], yo[:, 4 * n:4 * n + 4, :]).then_inc(s_out, 16)
            sp.wait_ge(s_yo[3], 2)
            sp.dma_start(out[:, 12:14, :], yo[:, 12:14, :]).then_inc(s_out, 16)
            sp.wait_ge(s_yo[2], 4)
            sp.dma_start(out[:, 8:12, :], yo[:, 8:12, :]).then_inc(s_out, 16)
            sp.wait_ge(s_yo[3], 4)
            sp.dma_start(out[:, 14:16, :], yo[:, 14:16, :]).then_inc(s_out, 16)
            sp.wait_ge(s_out, 16 * 5)

        @block.gpsimd
        def _(pool):
            for c in range(4):
                pool.memset(vaug[:, c, :, HD:HA], 1.0).then_inc(s_ones, 1)
            pool.sem_inc(s_x1l, 1)

            def outer(t, c, k):
                pool.wait_ge(s_fea, t + 1)
                pool.wait_ge(s_vev, t + 1)
                for h0, h1 in ((0, 6), (6, 16)):
                    m = h1 - h0
                    nc.gpsimd.tensor_tensor(
                        pr[:, k, h0:h1], fea[:, c, E + HD * h0:E + HD * h1].rearrange("p (h d) -> p h d", h=m)
                        .unsqueeze(2).to_broadcast([P, m, HA, HD]),
                        vaug[:, c, h0:h1].unsqueeze(3).to_broadcast([P, m, HA, HD]), ALU.mult).then_inc(s_pr, 1)

            def pairs(t, k):
                for n, (h0, h1) in enumerate(((0, 11), (11, 16))):
                    pool.wait_ge(s_qs, 3 * t + n + 2)
                    v = qs[:, k, h0:h1].rearrange("p h a d -> p (h a) d")
                    nc.gpsimd.tensor_tensor(hs[:, k, HA * h0:HA * h1], v[:, :, 0:HD // 2], v[:, :, HD // 2:HD],
                                            ALU.add).then_inc(s_hs, 1)

            def finish(b):
                pool.wait_ge(s_x1te, b + 1)
                pool.wait_ge(s_x1h, b + 1)
                nc.gpsimd.tensor_tensor(x1tl[:, ds(512 * b, 512)], x1ts[:, :],
                                        x1th[:, ds(512 * b, 512)].bitcast(f32), ALU.subtract)\
                    .then_inc(s_x1l, 1)

            def biased(b, s=0):
                pool.wait_ge(s_sig, b + 1)
                nc.gpsimd.tensor_tensor(sfc[:, :, :].rearrange("p (t g) e -> p t (g e)", t=TPB), sc[:, s, :, :],
                                        bias[:, :].unsqueeze(1).to_broadcast([P, TPB, NE]), ALU.add)\
                    .then_inc(s_sfc, 1)

            def chosen(b):
                pool.wait_ge(s_rch, STEPS * b + 4)
                nc.gpsimd.tensor_tensor(sg4[:, :, :], sfc[:, :, :],
                                        gm[:, :].unsqueeze(2).to_broadcast([P, TPB * GROUPS, GE]), ALU.mult)\
                    .then_inc(s_sg4, 1)

            def split_weights(ci, k):
                pool.wait_ge(s_wh, ci + 1)
                nc.gpsimd.tensor_tensor(wl[:, k, :], raw[:, k, :], wh[:, k, :].bitcast(f32),
                                        ALU.subtract).then_inc(s_wl, 1)

            def slot(b, c, kind):
                t = 4 * b + c
                if not (kind == LAST and c >= 2):
                    outer(t + 2, (c + 2) % 4, c % 2)
                if c == 3 and kind != FIRST:
                    biased(b - 1)
                if c == 0 and kind == INNER:
                    chosen(b - 2)
                if not (kind == LAST and c == 3):
                    pairs(t + 1, (c + 1) % 2)
                if c == 2 and kind != FIRST:
                    finish(b - 1)

            outer(0, 0, 0)
            outer(1, 1, 1)
            pairs(0, 0)
            pool.wait_ge(s_small, 48)
            for c in range(4):
                slot(0, c, FIRST)
            slot(1, 0, SECOND)
            with pool.Fori(1, BATCH - 1) as b:
                for c in (1, 2, 3):
                    slot(b, c, INNER)
                slot(b + 1, 0, INNER)
            slot(BATCH - 1, 1, LAST)
            slot(BATCH - 1, 2, LAST)
            for ci in range(AHEAD):
                split_weights(ci, ci)
            slot(BATCH - 1, 3, LAST)

            def lower(ci, n):
                pool.wait_ge(s_hhi, 4 * ci + n + 1)
                nc.gpsimd.tensor_tensor(hlo[:, n, :], hh[:, n, :], hhi[:, n, :].bitcast(f32),
                                        ALU.subtract).then_inc(s_hlo, 1)

            def chunk(ci, j, last=False, units=QB):
                for n in range(units):
                    if n == 1 and not last:
                        split_weights(ci + AHEAD, (j + AHEAD) % SLOTS)
                    lower(ci, n)

            chosen(BATCH - 2)
            for n in range(3):
                lower(0, n)
            finish(BATCH - 1)
            biased(BATCH - 1, 1)
            lower(0, 3)
            split_weights(2, 2)
            lower(1, 0)
            lower(1, 1)
            split_weights(3, 3)
            lower(1, 2)
            lower(1, 3)
            with pool.Fori(0, ROUNDS - 1) as i:
                for j in range(SC, SC + SLOTS):
                    chunk(SLOTS * i + j, j)
            for ci in range(NCH - SLOTS, NCH):
                chunk(ci, ci, ci >= NCH - AHEAD, QB - (ci == NCH - 1))

        @block.scalar
        def _(act):
            act.dma_start(wqkv[:, :], w_qkv).then_inc(s_wqkv, 16)
            act.wait_ge(s_ones, 4)
            nc.scalar.activation(warm[:, :], vaug[:, 0, 0, HD:HA], ACT.Exp).then_inc(s_warm, 1)

            def exps(t, c, queried=None, src=pj):
                act.wait_ge(s_proj, t + 1)
                if queried is not None:
                    act.wait_ge(s_qt, queried)
                nc.scalar.activation(ex[:, c, :], src[:, 0:2 * E], ACT.Exp).then_inc(s_ex, 1)
                nc.scalar.activation(re[:, c, :], src[:, 0:2 * E], ACT.Relu).then_inc(s_re, 1)
                nc.scalar.activation(vaug[:, c, :, 0:HD],
                                     src[:, 2 * E:3 * E].rearrange("p (h d) -> p h d", h=HEADS), ACT.Copy)\
                    .then_inc(s_vev, 1)

            def query(t, k):
                act.wait_ge(s_qt, t + 1)
                nc.scalar.activation(qt[:, k, :], qtb, ACT.Copy).then_inc(s_qte, 1)

            def out_transpose(t, k):
                act.wait_ge(s_aot, t + 1)
                nc.scalar.activation(aot[:, k, :], tbk[:, 0:P], ACT.Copy).then_inc(s_aote, 1)

            def residual(t, c):
                act.wait_ge(s_y, t + 1)
                nc.scalar.activation(xa[:, c, :], tbk[:, P:2 * P], ACT.Copy).then_inc(s_xa, 1)

            def deviation(b):
                act.wait_ge(s_vare, b + 1)
                nc.scalar.activation(std[:, :], vare[:, :], ACT.Sqrt).then_inc(s_std, 1)

            def normalise(b, c0, c1):
                act.wait_ge(s_shift, b + 1)
                for c in range(c0, c1):
                    nc.scalar.activation(x1s[:, c, :], xa[:, c, :], ACT.Identity, bias=shift[:, c:c + 1],
                                         scale=rstd[:, c:c + 1]).then_inc(s_x1, 1)

            def x1_transpose(b, src):
                act.wait_ge(s_x1t, b + 1)
                act.wait_ge(s_x1l, b + 1)
                nc.scalar.activation(x1ts[:, :], src[:, :], ACT.Copy).then_inc(s_x1te, 1)
                nc.scalar.activation(x1th[:, ds(512 * b, 512)], src[:, :], ACT.Copy).then_inc(s_x1h, 1)

            def scores(b, src, s=0):
                act.wait_ge(s_lg, b + 1)
                nc.scalar.activation(sc[:, s, :, :], src[:, 0:4 * NE].rearrange("p (c e) -> p c e", c=4), ACT.Sigmoid)\
                    .then_inc(s_sig, 1)

            def weights(b, src):
                act.wait_ge(s_rtt, b + 1)
                nc.scalar.activation(rt[:, ds(512 * b, 512)], src[:, :], ACT.Copy).then_inc(s_rte, 1)

            def split_weights(ci, k, loaded):
                act.wait_ge(s_raw[k], loaded)
                nc.scalar.activation(wh[:, k, :], raw[:, k, :], ACT.Copy).then_inc(s_wh, 1)

            def upper(u, n):
                act.wait_ge(s_h, u + 1)
                nc.scalar.activation(hhi[:, n, :], hh[:, n, :], ACT.Copy).then_inc(s_hhi, 1)

            def slot(b, c, kind):
                t = 4 * b + c
                if c == 3 and kind != FIRST:
                    scores(b - 1, bbk)
                if kind != LAST:
                    exps(t + 3, (c + 3) % 4, t + 2)
                if not (kind == LAST and c == 3):
                    query(t + 1, (c + 1) % 2)
                if c == 1 and kind != FIRST:
                    deviation(b - 1)
                if not (kind == FIRST and c == 0):
                    out_transpose(t - 1, (c + 1) % 2)
                if c == 1 and kind != FIRST:
                    normalise(b - 1, 0, 1)
                if c == 2 and kind != FIRST:
                    x1_transpose(b - 1, bbk)
                if c == 1 and kind != FIRST:
                    act.wait_ge(s_x1, 4 * b - 3)
                if not (kind == FIRST and c == 0):
                    residual(t - 1, (c + 3) % 4)
                if c == 1 and kind != FIRST:
                    normalise(b - 1, 1, 4)

            exps(0, 0)
            exps(1, 1, src=bbk)
            exps(2, 2, src=ob)
            query(0, 0)
            act.wait_ge(s_cst, 16)
            nc.scalar.activation(identr[:, :], ident, ACT.Copy).then_inc(s_idr, 1)
            for c in range(4):
                slot(0, c, FIRST)
            slot(1, 0, SECOND)
            with act.Fori(1, BATCH - 1) as b:
                for c in (1, 2, 3):
                    slot(b, c, INNER)
                slot(b + 1, 0, INNER)
            slot(BATCH - 1, 1, LAST)
            slot(BATCH - 1, 2, LAST)
            for ci in range(AHEAD):
                split_weights(ci, ci, 16)
            slot(BATCH - 1, 3, LAST)

            def silu(u, n, shared=False):
                act.wait_ge(s_g, u + 1)
                nc.scalar.activation(ug[:, n, :] if shared else gbk[n % 2][:, :], gbk[n % 2][:, :], ACT.Silu)\
                    .then_inc(s_silu, 1)

            def chunk(ci, j, i, last=False, weigh=False):
                for n in range(QB):
                    silu(4 * ci + n, n)
                    if n == 0 and not last:
                        split_weights(ci + AHEAD, (j + AHEAD) % SLOTS, 16 * (i + (j + AHEAD) // SLOTS + 1))
                    upper(4 * ci + n - 1, (n + 3) % 4)
                    if n == 2 and weigh:
                        weights(BATCH - 1, ubk[1])

            silu(0, 0, shared=True)
            silu(1, 1, shared=True)
            out_transpose(NT - 1, 1)
            weights(0, sbk)
            upper(0, 0)
            residual(NT - 1, 3)
            weights(1, ob)
            upper(1, 1)
            silu(2, 2, shared=True)
            deviation(BATCH - 1)
            normalise(BATCH - 1, 0, 2)
            upper(2, 2)
            x1_transpose(BATCH - 1, tbk)
            scores(BATCH - 1, gbk[1], 1)
            weights(BATCH - 2, ubk[1])
            for u in range(3, 4 * SC):
                silu(u, u % 4, shared=True)
                if u in (4, 6):
                    split_weights(u // 2, u // 2, 16)
                if u > 3:
                    upper(u - 1, (u - 1) % 4)
            for j in range(SC, SC + SLOTS):
                chunk(j, j, 0, weigh=j == SC)
            with act.Fori(1, ROUNDS - 1) as i:
                for j in range(SC, SC + SLOTS):
                    chunk(SLOTS * i + j, j, i)
            for j in range(SC, SC + SLOTS):
                ci = SLOTS * (ROUNDS - 1) + j
                chunk(ci, j, ROUNDS - 1, last=ci >= NCH - AHEAD)
            upper(4 * NCH - 1, 3)

            def sums_out(n):
                act.wait_ge(s_d, 4 * NCH - 3 + n)
                nc.scalar.activation(osb[:, n, :], ou[n][:, :], ACT.Copy).then_inc(s_osb[n], 1)

            def deviation2(n):
                act.wait_ge(s_va2, n + 1)
                nc.scalar.activation(std2[:, 4 * n:4 * n + 4], vare2[:, 4 * n:4 * n + 4], ACT.Sqrt)\
                    .then_inc(s_sd2, 1)

            def normalise2(n):
                act.wait_ge(s_sh2, n + 1)
                for t in range(4 * n, 4 * n + 4):
                    c = t % 4
                    nc.scalar.activation(yo[:, t, :], tails[n][:, P * c:P * c + P], ACT.Identity,
                                         bias=shift2[:, t:t + 1], scale=rstd2[:, t:t + 1]).then_inc(s_yo[n], 1)

            sums_out(1)
            sums_out(2)
            deviation2(0)
            sums_out(3)
            deviation2(1)
            normalise2(0)
            deviation2(2)
            normalise2(1)
            deviation2(3)
            normalise2(3)

        @block.vector
        def _(dve):
            V = nc.vector

            def elu(t, c):
                dve.wait_ge(s_re, t + 1)
                V.scalar_tensor_tensor(fea[:, c, :], ex[:, c, :], 1.0, re[:, c, :], ALU.min, ALU.add)\
                    .then_inc(s_fea, 1)

            def times_q(t, c, k, j):
                h0, m = THIRDS[j]
                dve.wait_ge(s_cum, 3 * t + j + 1)
                V.tensor_tensor(qs[:, k, h0:h0 + m],
                                cum[j][:, 0:HP * m].rearrange("p (h a d) -> p h a d", h=m, a=HA),
                                fea[:, c, HD * h0:HD * (h0 + m)].rearrange("p (h d) -> p h d", h=m)
                                .unsqueeze(2).to_broadcast([P, m, HA, HD]), ALU.mult).then_inc(s_qs, 1)

            def state(b, c):
                dve.wait_ge(s_st, 3 * b + c + 1)
                V.tensor_tensor(sm[:, c, :], sbk[:, 0:HEADS * HA], bmask, ALU.mult).then_inc(s_sm, 1)

            def total(t, k):
                dve.wait_ge(s_hs, 2 * t + 2)
                V.tensor_reduce(num[:, k].rearrange("p h a -> p (h a)"), hs[:, k], AX.X, ALU.add)\
                    .then_inc(s_num, 1)

            def with_state(t, b, c, k):
                dve.wait_ge(s_num, t + 1)
                if c:
                    dve.wait_ge(s_o, 3 * b + c)
                    V.tensor_tensor(nsum[:, k], ob[:, 0:HEADS * HA].rearrange("p (h a) -> p h a", h=HEADS),
                                    num[:, k], ALU.add).then_inc(s_nsum, 1)

            def denominator(b, c, k):
                if c:
                    dve.wait_ge(s_nsum, 3 * b + c)
                o = nsum[:, k] if c else num[:, k]
                V.tensor_scalar(den[:, k, :].unsqueeze(2), o[:, :, HD:HA], 1e-6, None, ALU.max).then_inc(s_den, 1)

            def reciprocal(t, k):
                dve.wait_ge(s_den, t + 1)
                V.reciprocal(rden[:, k, :], den[:, k, :]).then_inc(s_rden, 1)

            def divide(t, c, k):
                dve.wait_ge(s_rden, t + 1)
                o = nsum[:, k] if c else num[:, k]
                V.tensor_tensor(ao[:, k, :].rearrange("p (h d) -> p h d", h=HEADS), o[:, :, 0:HD],
                                rden[:, k, :].unsqueeze(2).to_broadcast([P, HEADS, HD]), ALU.mult)\
                    .then_inc(s_ao, 1)

            def statistics(t, c):
                dve.wait_ge(s_xa, t + 1)
                V.bn_stats(bns[:, c, :], xa[:, c, :]).then_inc(s_bn, 1)

            def variance(b):
                half = E // 2
                dve.wait_ge(s_bn, 4 * b + 4)
                V.tensor_tensor(st[:, :, 0:1], bns[:, :, 1:2], bns[:, :, 4:5], ALU.add).then_inc(s_mv, 1)
                V.tensor_tensor(st[:, :, 1:2], bns[:, :, 1:2], bns[:, :, 4:5], ALU.subtract).then_inc(s_mv, 1)
                V.tensor_tensor(st[:, :, 2:3], bns[:, :, 2:3], bns[:, :, 5:6], ALU.add).then_inc(s_mv, 1)
                dve.wait_ge(s_mv, 6 * b + 3)
                V.tensor_scalar(mean[:, :].unsqueeze(2), st[:, :, 0:1], 0.5, None, ALU.mult).then_inc(s_mv, 1)
                V.tensor_tensor(st[:, :, 3:4], st[:, :, 1:2], st[:, :, 1:2], ALU.mult).then_inc(s_mv, 1)
                V.tensor_scalar(st[:, :, 4:5], st[:, :, 2:3], 0.5 / half, 1e-5, ALU.mult, ALU.add).then_inc(s_mv, 1)
                dve.wait_ge(s_mv, 6 * b + 6)
                V.scalar_tensor_tensor(vare[:, :].unsqueeze(2), st[:, :, 3:4], 0.25, st[:, :, 4:5],
                                       ALU.mult, ALU.add).then_inc(s_vare, 1)

            def scale(b):
                dve.wait_ge(s_std, b + 1)
                V.reciprocal(rstd[:, :], std[:, :]).then_inc(s_rstd, 1)

            def shifts(b):
                dve.wait_ge(s_rstd, b + 1)
                V.scalar_tensor_tensor(shift[:, :], mean[:, :], -1.0, rstd[:, :], ALU.mult, ALU.mult)\
                    .then_inc(s_shift, 1)

            def add(ins):
                ins.then_inc(s_rch, 1)

            def settled(signal, value):
                dve.wait_ge(signal, value)
                dve.sem_inc(s_settled, 1)

            GSTEPS = 11

            def pairwise(out_, a, b_, op):
                V.tensor_tensor(out_, a, b_, op).then_inc(s_grp, 1)

            def group_1(b):
                dve.wait_ge(s_sfc, b + 1)
                pairwise(ta[:, :, :], sfc[:, :, 0:4], sfc[:, :, 4:8], ALU.max)
                pairwise(tb[:, :, :], sfc[:, :, 0:4], sfc[:, :, 4:8], ALU.min)

            def group_2(b):
                dve.wait_ge(s_grp, GSTEPS * b + 2)
                pairwise(tc[:, :, :], ta[:, :, 0:2], ta[:, :, 2:4], ALU.max)
                pairwise(td[:, :, :], ta[:, :, 0:2], ta[:, :, 2:4], ALU.min)
                pairwise(te[:, :, :], tb[:, :, 0:2], tb[:, :, 2:4], ALU.max)

            def group_3(b):
                dve.wait_ge(s_grp, GSTEPS * b + 5)
                pairwise(te[:, :, :], te[:, :, :], td[:, :, :], ALU.max)
                pairwise(ta[:, :, 0:1], tc[:, :, 0:1], tc[:, :, 1:2], ALU.max)
                pairwise(tb[:, :, 0:1], tc[:, :, 0:1], tc[:, :, 1:2], ALU.min)

            def group_4(b):
                dve.wait_ge(s_grp, GSTEPS * b + 8)
                pairwise(tf[:, :, :], te[:, :, 0:1], te[:, :, 1:2], ALU.max)

            def group_5(b):
                dve.wait_ge(s_grp, GSTEPS * b + 9)
                pairwise(tb[:, :, 0:1], tb[:, :, 0:1], tf[:, :, :], ALU.max)

            def group_6(b):
                dve.wait_ge(s_grp, GSTEPS * b + 10)
                pairwise(gs[:, :, :].rearrange("p t g -> p (t g)").unsqueeze(2), ta[:, :, 0:1], tb[:, :, 0:1], ALU.add)

            def route_1(b):
                settled(s_grp, GSTEPS * b + GSTEPS)
                for c in range(TPB):
                    last = V.max(gtop[:, c, :], gs[:, c, :])
                add(last)

            def route_2(b):
                dve.wait_ge(s_rch, STEPS * b + 1)
                add(V.tensor_copy(gtake[:, :, 0:TOPG], gtop[:, :, 0:TOPG]))

            def route_3(b):
                settled(s_rch, STEPS * b + 2)
                for c in range(TPB):
                    last = V.match_replace(gleft[:, c, :], gtake[:, c, :], gs[:, c, :], NONE)
                add(last)

            def route_4(b):
                dve.wait_ge(s_rch, STEPS * b + 3)
                add(V.tensor_scalar(gm[:, :], gleft[:, :, :].rearrange("p t g -> p (t g)"), NONE, None, ALU.is_equal))

            def route_5(b):
                dve.wait_ge(s_sg4, b + 1)
                add(V.tensor_scalar(sg4[:, :, :], sg4[:, :, :], 0.0, None, ALU.add))

            sview = sg4[:, :, :].rearrange("p (t g) e -> p t (g e)", t=TPB)

            def route_6(b):
                settled(s_rch, STEPS * b + 5)
                for c in range(TPB):
                    last = V.max(top[:, c, :], sview[:, c, :])
                add(last)

            def route_7(b):
                settled(s_rch, STEPS * b + 6)
                for c in range(TPB):
                    last = V.match_replace(left[:, c, :], top[:, c, :], sview[:, c, :], NONE)
                add(last)

            def route_8(b, s=0):
                dve.wait_ge(s_rch, STEPS * b + 7)
                add(V.scalar_tensor_tensor(wt[:, :, :], left[:, :, :], NONE, sc[:, s, :, :], ALU.is_equal, ALU.mult))

            def route_9(b):
                dve.wait_ge(s_rch, STEPS * b + 8)
                add(V.tensor_reduce(wsum[:, 0, :], wt[:, :, :], AX.X, ALU.add))

            def route_10(b):
                dve.wait_ge(s_rch, STEPS * b + 9)
                add(V.tensor_scalar(wsum[:, 1, :], wsum[:, 0, :], 1e-20, None, ALU.add))

            def route_11(b):
                dve.wait_ge(s_rch, STEPS * b + 10)
                add(V.reciprocal(wsum[:, 2, :], wsum[:, 1, :]))

            def route_12(b):
                dve.wait_ge(s_rch, STEPS * b + 11)
                add(V.scalar_tensor_tensor(wt[:, :, :], wt[:, :, :], RSCALE,
                                           wsum[:, 2, :].unsqueeze(2).to_broadcast([P, TPB, NE]),
                                           ALU.mult, ALU.mult))

            def route_13(b):
                dve.wait_ge(s_rch, STEPS * b + 12)
                V.tensor_copy(rwd[:, ds(TPB * b, TPB), :, :], wt[:, :, :].unsqueeze(3).to_broadcast([P, TPB, NE, RPC]))\
                    .then_inc(s_rw, 1)

            def slot(b, c, kind):
                t = 4 * b + c
                k, c1, k1 = c % 2, (c + 1) % 4, (c + 1) % 2
                norm = kind != FIRST
                groups = c == 3 and norm
                experts = c == 0 and kind == INNER
                running = not (kind == LAST and c == 3)
                if not (kind == LAST and c >= 2):
                    elu(t + 2, (c + 2) % 4)
                if c < 3:
                    state(b, c)
                total(t, k)
                if experts:
                    route_3(b - 2)
                with_state(t, b, c, k)
                if experts:
                    route_4(b - 2)
                if running:
                    times_q(t + 1, c1, k1, 0)
                denominator(b, c, k)
                if c == 1 and norm:
                    scale(b - 1)
                if running:
                    times_q(t + 1, c1, k1, 1)
                if c == 1 and norm:
                    shifts(b - 1)
                if experts:
                    route_5(b - 2)
                reciprocal(t, k)
                if running:
                    times_q(t + 1, c1, k1, 2)
                if experts:
                    route_6(b - 2)
                divide(t, c, k)
                if experts:
                    route_7(b - 2)
                if groups:
                    group_1(b - 1)
                    group_2(b - 1)
                if experts:
                    route_8(b - 2)
                if not (kind == FIRST and c == 0):
                    statistics(t - 1, (c + 3) % 4)
                if groups:
                    group_3(b - 1)
                    group_4(b - 1)
                    group_5(b - 1)
                if c == 0 and norm:
                    variance(b - 1)
                if experts:
                    route_9(b - 2)
                    route_10(b - 2)
                    route_11(b - 2)
                    route_12(b - 2)
                    route_13(b - 2)
                if groups:
                    group_6(b - 1)
                    route_1(b - 1)
                    route_2(b - 1)

            V.memset(gtake[:, :, TOPG:GROUPS], -NONE)
            elu(0, 0)
            elu(1, 1)
            for j in range(3):
                times_q(0, 0, 0, j)
            dve.wait_ge(s_cst, 16)
            for c in range(4):
                slot(0, c, FIRST)
            slot(1, 0, SECOND)
            with dve.Fori(1, BATCH - 1) as b:
                for c in (1, 2, 3):
                    slot(b, c, INNER)
                slot(b + 1, 0, INNER)
            for c in (1, 2, 3):
                slot(BATCH - 1, c, LAST)

            def shared_unit(u):
                n = u % 4
                dve.wait_ge(s_silu, u + 1)
                dve.wait_ge(s_u, u + 1)
                V.tensor_tensor(hh[:, n, :], ubk[n % 2][:, :], ug[:, n, :], ALU.mult).then_inc(s_h, 1)

            def chosen(b):
                dve.wait_ge(s_rch, STEPS * b + 4)
                V.tensor_tensor(sg4[:, :, :], sfc[:, :, :],
                                gm[:, :].unsqueeze(2).to_broadcast([P, TPB * GROUPS, GE]), ALU.mult)\
                    .then_inc(s_sg4, 1)

            before, last = BATCH - 2, BATCH - 1
            shared_unit(0)
            route_3(before)
            route_4(before)
            shared_unit(1)
            statistics(NT - 1, 3)
            variance(last)
            route_5(before)
            scale(last)
            shifts(last)
            for c in range(2, 4):
                V.tensor_scalar(x1s[:, c, :], xa[:, c, :], mean[:, c:c + 1], rstd[:, c:c + 1],
                                ALU.subtract, ALU.mult).then_inc(s_x1, 1)
            route_6(before)
            shared_unit(2)
            route_7(before)
            route_8(before)
            route_9(before)
            route_10(before)
            route_11(before)
            route_12(before)
            route_13(before)
            group_1(last)
            group_2(last)
            group_3(last)
            group_4(last)
            group_5(last)
            group_6(last)
            route_1(last)
            route_2(last)
            shared_unit(3)
            route_3(last)
            route_4(last)
            shared_unit(4)
            chosen(last)
            route_5(last)
            route_6(last)
            shared_unit(5)
            route_7(last)
            route_8(last, 1)
            shared_unit(6)
            route_9(last)
            route_10(last)
            route_11(last)
            shared_unit(7)
            route_12(last)
            route_13(last)

            def chunk(ci, first=False):
                for n in range(QB):
                    u = 4 * ci + n
                    if first and n >= 2:
                        dve.wait_ge(s_rte, n + 1)
                    dve.wait_ge(s_u, u + 1)
                    V.tensor_tensor(ug[:, n, :], ubk[n % 2][:, :], rt[:, 512 * n:512 * n + 512], ALU.mult)\
                        .then_inc(s_ur, 1)
                    dve.wait_ge(s_ur, u + 1 - 4 * SC)
                    dve.wait_ge(s_silu, u + 1)
                    V.tensor_tensor(hh[:, n, :], gbk[n % 2][:, :], ug[:, n, :], ALU.mult).then_inc(s_h, 1)

            dve.wait_ge(s_rte, 2)
            for ci in range(SC, SC + SLOTS):
                chunk(ci, ci == SC)
            with dve.Fori(1, ROUNDS) as i:
                for j in range(SC, SC + SLOTS):
                    chunk(SLOTS * i + j)

            dve.wait_ge(s_d, 4 * NCH - 3)
            V.tensor_copy(osb[:, 0, :], ou[0][:, :]).then_inc(s_osb[0], 1)
            dve.wait_ge(s_hhi, 4 * NCH)
            V.tensor_tensor(hlo[:, 3, :], hh[:, 3, :], hhi[:, 3, :].bitcast(f32), ALU.subtract).then_inc(s_hlo2, 1)

            def variance2(n):
                q = slice(4 * n, 4 * n + 4)
                dve.wait_ge(s_ot, n + 1)
                for t in range(4 * n, 4 * n + 4):
                    c = t % 4
                    V.bn_stats(bns2[:, t, :], tails[n][:, P * c:P * c + P]).then_inc(s_bn2, 1)
                for t in range(4 * n, 4 * n + 4):
                    dve.wait_ge(s_bn2, t + 1)
                    V.bn_aggr(mv2[:, t, :], bns2[:, t, :]).then_inc(s_mv2, 1)
                dve.wait_ge(s_mv2, 4 * n + 4)
                V.tensor_scalar(vare2[:, q].unsqueeze(2), mv2[:, q, 1:2], 1e-5, None, ALU.add).then_inc(s_va2, 1)

            def scale2(n):
                q = slice(4 * n, 4 * n + 4)
                dve.wait_ge(s_sd2, n + 1)
                V.reciprocal(rstd2[:, q], std2[:, q]).then_inc(s_rs2, 1)
                dve.wait_ge(s_rs2, n + 1)
                V.scalar_tensor_tensor(shift2[:, q].unsqueeze(2), mv2[:, q, 0:1], -1.0, rstd2[:, q].unsqueeze(2),
                                       ALU.mult, ALU.mult).then_inc(s_sh2, 1)

            variance2(0)
            for n in range(1, QB):
                variance2(n)
                scale2(n - 1)
            scale2(QB - 1)
            for t in range(8, 12):
                c = t % 4
                V.tensor_scalar(yo[:, t, :], tails[2][:, P * c:P * c + P], mv2[:, t, 0:1], rstd2[:, t:t + 1],
                                ALU.subtract, ALU.mult).then_inc(s_yo[2], 1)

        @block.tensor
        def _(pe):
            mm = nc.tensor.matmul

            def project(t, c, nth, dst=pj, t_query=None):
                if nth is None:
                    pe.wait_ge(s_x4, 16)
                else:
                    pe.wait_ge(s_xt[c], 16 * nth)
                if t_query is not None:
                    pe.wait_ge(s_vev, t)
                    pe.wait_ge(s_qte, t_query)
                mm(dst[:, 0:3 * E], xt[:, c, :], wqkv[:, :], start=True, stop=True).then_inc(s_proj, 1)

            def query(t, c):
                pe.wait_ge(s_fea, t + 1)
                nc.tensor.transpose(qtb, fea[:, c, 0:E], ident).then_inc(s_qt, 1)

            def running(t, k, j, first=False):
                h0, m = THIRDS[j]
                if j < 2:
                    pe.wait_ge(s_pr, 2 * t + j + 1)
                if not first:
                    pe.wait_ge(s_qs, 3 * t + j - 2)
                mm(cum[j][:, 0:HP * m], causal, pr[:, k, h0:h0 + m].rearrange("p h a d -> p (h a d)"),
                   start=True, stop=True).then_inc(s_cum, 1)

            def sums(b, c, first):
                t = 4 * b + c
                if c:
                    pe.wait_ge(s_qte, t + 1)
                    pe.wait_ge(s_sm, 3 * b + c)
                    if not (first and c == 1):
                        pe.wait_ge(s_nsum, 3 * b + c - 1)
                    mm(ob[:, 0:HEADS * HA], qt[:, c % 2, :], sm[:, c - 1, :], start=True, stop=True)\
                        .then_inc(s_o, 1)
                if c < 3:
                    if c == 0 and not first:
                        pe.wait_ge(s_sm, 3 * b)
                    elif c == 0:
                        pe.wait_ge(s_vev, t + 1)
                        pe.wait_ge(s_fea, t + 1)
                    mm(sbk[:, 0:HEADS * HA], fea[:, c, E:2 * E],
                       vaug[:, c].rearrange("p h a -> p (h a)"), start=(c == 0), stop=True,
                       skip_group_check=True).then_inc(s_st, 1)

            def out_transpose(t, k, first=False):
                pe.wait_ge(s_ao, t + 1)
                if not first:
                    pe.wait_ge(s_xa, t)
                nc.tensor.transpose(tbk[:, 0:P], ao[:, k, :], ident).then_inc(s_aot, 1)

            def output(t, k):
                pe.wait_ge(s_aote, t + 1)
                mm(tbk[:, P:2 * P], ident, xtok[:, ds(t, 1), :].rearrange("p a e -> p (a e)"), start=True, stop=False)
                mm(tbk[:, P:2 * P], aot[:, k, :], wo[:, :], start=False, stop=True).then_inc(s_y, 1)

            def x1_transpose(b, dst):
                pe.wait_ge(s_x1, 4 * b + 4)
                for c in range(4):
                    last = nc.tensor.transpose(dst[:, P * c:P * c + P], x1s[:, c, :], ident)
                last.then_inc(s_x1t, 1)

            def logits(b, dst, apart=False):
                pe.wait_ge(s_x1te, b + 1)
                if not apart:
                    pe.wait_ge(s_x1h, b + 1)
                for c in range(4):
                    last = mm(dst[:, NE * c:NE * c + NE], x1ts[:, P * c:P * c + P], gw[:, :], start=True, stop=True)
                last.then_inc(s_lg, 1)

            def weights(b, dst):
                pe.wait_ge(s_rw, b + 1)
                for c in range(4):
                    last = nc.tensor.transpose(dst[:, P * c:P * c + P],
                                               rwd[:, TPB * b + c].rearrange("p e r -> p (e r)"), ident)
                last.then_inc(s_rtt, 1)

            def slot(b, c, kind):
                t = 4 * b + c
                if kind != LAST:
                    project(t + 3, (c + 3) % 4, None if kind == FIRST and c == 0 else b + (c >= 1), pj, t + 1)
                if not (kind == LAST and c == 3):
                    if kind == LAST:
                        pe.wait_ge(s_vev, NT)
                        pe.wait_ge(s_qte, t + 1)
                    query(t + 1, (c + 1) % 4)
                sums(b, c, kind == FIRST)
                if not (kind == LAST and c == 3):
                    running(t + 1, (c + 1) % 2, 0)
                if not (kind == LAST and c == 3):
                    running(t + 1, (c + 1) % 2, 1)
                if not (kind == LAST and c == 3):
                    running(t + 1, (c + 1) % 2, 2)
                if not (kind == FIRST and c == 0):
                    out_transpose(t - 1, (c + 1) % 2, kind == FIRST and c == 1)
                if c == 2 and kind != FIRST:
                    x1_transpose(b - 1, bbk)
                if not (kind == FIRST and c == 0):
                    output(t - 1, (c + 1) % 2)
                if c == 2 and kind != FIRST:
                    logits(b - 1, bbk)

            pe.wait_ge(s_wqkv, 16)
            project(0, 0, None)
            project(1, 1, None, bbk)
            project(2, 2, None, ob)
            pe.wait_ge(s_cst, 16)
            pe.wait_ge(s_vev, 3)
            query(0, 0)
            for j in range(3):
                running(0, 0, j, True)
            pe.wait_ge(s_small, 48)
            pe.wait_ge(s_xtok, 16)
            for c in range(4):
                slot(0, c, FIRST)
            slot(1, 0, SECOND)
            with pe.Fori(1, BATCH - 1) as b:
                for c in (1, 2, 3):
                    slot(b, c, INNER)
                slot(b + 1, 0, INNER)
            for c in (1, 2, 3):
                slot(BATCH - 1, c, LAST)

            def product(dst, k, col, hi, lo, start, stop):
                mm(dst, wh[:, k, col:col + P], hi, start=start, stop=False, skip_group_check=True)
                mm(dst, wh[:, k, col:col + P], lo, start=False, stop=False, skip_group_check=True)
                return mm(dst, wl[:, k, col:col + P], hi, start=False, stop=stop, skip_group_check=True)

            def down(u, k, n, last=False):
                if last:
                    pe.wait_ge(s_hlo2, 1)
                else:
                    pe.wait_ge(s_hlo, u + 1)
                product(ou[n][:, :], k, 2 * P, hhi[:, n, :], hlo[:, n, :], False, True).then_inc(s_d, 1)

            LAG = 3

            def gate(k, n):
                xs = slice(512 * n, 512 * n + 512)
                product(gbk[n % 2][:, :], k, 0, x1th[:, xs], x1tl[:, xs], True, True).then_inc(s_g, 1)

            def up(k, n):
                xs = slice(512 * n, 512 * n + 512)
                product(ubk[n % 2][:, :], k, P, x1th[:, xs], x1tl[:, xs], True, True).then_inc(s_u, 1)

            def residual(n):
                xs = slice(512 * n, 512 * n + 512)
                if n == 0:
                    pe.wait_ge(s_idr, 1)
                    pe.wait_ge(s_vev, NT)
                elif n == 1:
                    pe.wait_ge(s_rte, 1)
                elif n == 2:
                    pe.wait_ge(s_rte, 2)
                else:
                    pe.wait_ge(s_x1h, BATCH)
                mm(ou[n][:, :], identr[:, :], x1th[:, xs], start=True, stop=False, skip_group_check=True)
                mm(ou[n][:, :], identr[:, :], x1tl[:, xs], start=False, stop=False, skip_group_check=True)

            def chunk(ci, j, n0=0, weigh=False):
                pe.wait_ge(s_wh, ci + 1)
                pe.wait_ge(s_wl, ci + 1)
                for n in range(n0, QB):
                    u = 4 * ci + n
                    if j == 0 and n == 3:
                        residual(3)
                    pe.wait_ge(s_h, u - 1)
                    if n == 3 and weigh:
                        weights(BATCH - 1, ubk[1])
                    gate(j % SLOTS, n)
                    if n == 3 and weigh:
                        pe.wait_ge(s_rte, BATCH)
                    up(j % SLOTS, n)
                    if 4 * j + n >= LAG:
                        down(u - LAG, (4 * j + n - LAG) // 4 % SLOTS, (n - LAG) % 4)

            pe.wait_ge(s_qs, 3 * NT)
            pe.wait_ge(s_x1l, BATCH)
            pe.wait_ge(s_wl, 1)
            gate(0, 0)
            up(0, 0)
            pe.wait_ge(s_sig, BATCH - 1)
            gate(0, 1)
            up(0, 1)
            out_transpose(NT - 1, 1)
            pe.wait_ge(s_sm, 3 * BATCH)
            weights(0, sbk)
            residual(0)
            output(NT - 1, 1)
            pe.wait_ge(s_nsum, 3 * BATCH)
            weights(1, ob)
            pe.wait_ge(s_h, 1)
            gate(0, 2)
            up(0, 2)
            residual(1)
            residual(2)
            x1_transpose(BATCH - 1, tbk)
            logits(BATCH - 1, gbk[1], apart=True)
            pe.wait_ge(s_h, 2)
            weights(BATCH - 2, ubk[1])
            pe.wait_ge(s_x1l, BATCH + 1)
            pe.wait_ge(s_sig, BATCH)
            pe.wait_ge(s_rte, BATCH - 1)
            chunk(0, 0, 3)
            chunk(1, 1)
            for ci in range(SC, SC + SLOTS):
                chunk(ci, ci, weigh=ci == SC)
            with pe.Fori(1, ROUNDS) as i:
                for j in range(SC, SC + SLOTS):
                    chunk(SLOTS * i + j, j)

            def tail(n, hidden):
                pe.wait_ge(s_osb[n], 1)
                pe.wait_ge(s_h, hidden)
                for c in range(4):
                    last = nc.tensor.transpose(tails[n][:, P * c:P * c + P], osb[:, n, P * c:P * c + P], ident)
                last.then_inc(s_ot, 1)

            down(4 * NCH - 3, 1, 1)
            tail(0, 4 * NCH - 1)
            down(4 * NCH - 2, 1, 2)
            tail(1, 4 * NCH - 1)
            down(4 * NCH - 1, 1, 3, last=True)
            tail(2, 4 * NCH)
            tail(3, 4 * NCH)


def layouts(L0_attn_x, L0_attn_W_qkv, L0_attn_W_out, L0_ffn_gate_w, L0_ffn_gate_bias, L0_ffn_Wg, L0_ffn_Wu,
            L0_ffn_Wd, L0_ffn_Sg, L0_ffn_Su, L0_ffn_Sd):
    import numpy as np

    x = np.asarray(L0_attn_x).reshape(TOK, E)
    chunks = np.zeros((NCH, P, CW), np.float32)

    def rows_to_columns(w, first, count, at):
        full = np.zeros((count * P, E), np.float32)
        full[:w.shape[0]] = w
        chunks[first:first + count, :, at:at + P] = full.reshape(count, P, E).transpose(0, 2, 1)

    rows_to_columns(np.asarray(L0_ffn_Sg), 0, SC, 0)
    rows_to_columns(np.asarray(L0_ffn_Su), 0, SC, P)
    for w, at in ((L0_ffn_Wg, 0), (L0_ffn_Wu, P)):
        by_chunk = np.asarray(w).reshape(NE, RC, RPC, E).transpose(1, 3, 0, 2)
        chunks[SC:, :, at:at + P] = by_chunk.reshape(RC, E, P)
    sd = np.zeros((SC * P, E), np.float32)
    sd[:SHARED] = np.asarray(L0_ffn_Sd).T
    chunks[0:SC, :, 2 * P:3 * P] = sd.reshape(SC, P, E)
    by_chunk = np.asarray(L0_ffn_Wd).reshape(NE, E, RC, RPC).transpose(2, 0, 3, 1)
    chunks[SC:, :, 2 * P:3 * P] = by_chunk.reshape(RC, P, E)

    cst = np.zeros((P, C_END), np.float32)
    p = np.arange(P)
    scale = float(HD) ** -0.5
    cst[:, C_CAUSAL:C_CAUSAL + P] = (p[:, None] <= p[None, :]) * scale
    cst[:, C_BMASK:C_BMASK + HEADS * HA] = (p[:, None] // HD == np.arange(HEADS * HA)[None, :] // HA) * scale
    cst[:, C_IDENT:C_IDENT + P] = p[:, None] == p[None, :]
    return {
        "x_tok": np.ascontiguousarray(x.reshape(NT, P, E).transpose(1, 0, 2)),
        "x_t": np.ascontiguousarray(x.T),
        "w_qkv": np.ascontiguousarray(np.asarray(L0_attn_W_qkv).T),
        "w_out": np.ascontiguousarray(np.asarray(L0_attn_W_out).T),
        "gate_w": np.ascontiguousarray(np.asarray(L0_ffn_gate_w).T),
        "gate_bias": np.ascontiguousarray(np.broadcast_to(np.asarray(L0_ffn_gate_bias)[None, :], (P, NE))),
        "w_chunks": chunks,
        "consts": cst,
    }


def kernel(**inputs):
    import concourse.bacc as _bacc
    from concourse.bass_utils import run_bass_kernel_spmd as _run

    nc = _bacc.Bacc("TRN2", target_bir_lowering=False, num_devices=1)
    arrays, args = {}, []
    for name, a in layouts(**inputs).items():
        arrays[f"in_{name}"] = a
        args.append(nc.dram_tensor(f"in_{name}", a.shape, mybir.dt.from_np(a.dtype), kind="ExternalInput").ap())
    o = nc.dram_tensor("out_x", (BATCH, SEQ, E), mybir.dt.float32, kind="ExternalOutput").ap()
    build(nc, *args, o.rearrange("b (j p) e -> p (b j) e", p=P))
    r = _run(nc, [arrays], core_ids=[0])
    return r.results[0]["out_x"]
```
